# Optimizing a Trainium2 kernel written in Bass

```python
import numpy as np
import jax
import jax.numpy as jnp

def _softmax(x, axis=-1):
    return jax.nn.softmax(x, axis=axis)
def _gelu(x):
    return jax.nn.gelu(x, approximate=True)
def _silu(x):
    return jax.nn.silu(x)
def _sigmoid(x):
    return jax.nn.sigmoid(x)
def _layernorm(x, axis=-1, eps=1e-5):
    m = jnp.mean(x, axis=axis, keepdims=True)
    v = jnp.var(x, axis=axis, keepdims=True)
    return (x - m) / jnp.sqrt(v + eps)
def _scatter_add(tgt, idx, src, axis=0):
    return tgt.at[idx].add(src)
def _segment_sum(src, seg, n):
    return jax.ops.segment_sum(src, seg, n)

kernel_name = 'mk_adj_resnorm_d4_adj_128_ba4470'

def setup_inputs(seed: int = 0):
    np.random.seed(seed)
    _w = jnp.asarray
    def _rec_inputs():
        import jax
        import jax.numpy as jnp
        _gk = jax.random.key(seed)
        x = 0.0002279 + 0.9999 * jax.random.normal(jax.random.fold_in(_gk, 1), (2708, 128), jnp.float32)
        _w = (1.0 + jnp.arange(2708, dtype=jnp.float32)) ** -0.5
        _w = _w / _w.mean()
        _pij = jnp.clip(0.00590842 * _w[:, None] * _w[None, :], 0.0, 1.0)
        _a = jax.random.uniform(jax.random.fold_in(_gk, 2), (2708, 2708)) < _pij
        _a = jnp.logical_or(_a, jnp.swapaxes(_a, -1, -2))
        _af = _a.astype(jnp.float32)
        adj = _af
        return x, adj
    x, adj = _rec_inputs()
    def _L0_gnn_setup():
        import jax, jax.numpy as jnp
        import numpy as np
        N = 8192
        F = 128
        U = 128
        EDGE_P = 0.002

        def adj_norm(adj):
            a_hat = adj + jnp.eye(adj.shape[0], dtype=adj.dtype)
            d_inv_sqrt = jax.lax.rsqrt(jnp.sum(a_hat, axis=-1))
            return a_hat * d_inv_sqrt[:, None] * d_inv_sqrt[None, :]
        key = jax.random.key(seed)
        k1, k2, k3 = jax.random.split(key, 3)
        a = (jax.random.uniform(k1, (N, N)) < EDGE_P).astype(jnp.float32)
        adj = jnp.maximum(a, a.T)
        x = jax.random.normal(k2, (N, F), dtype=jnp.float32)
        W = jax.random.normal(k3, (F, U), dtype=jnp.float32) * 0.05
        b = jnp.zeros((U,), dtype=jnp.float32)
        return {'x': x, 'adj': adj, 'W': W, 'b': b}
    _L0_gnn_all = _L0_gnn_setup()
    _L0_gnn_in = {k: v for k, v in _L0_gnn_all.items() if k in ('W', 'b', )}
    del _L0_gnn_all

    def _L1_gnn_setup():
        import jax, jax.numpy as jnp
        import numpy as np
        N = 8192
        IN_DIM = 128
        OUT_DIM = 128
        DENSITY = 0.01
        key = jax.random.key(seed)
        kx, ka, kw, ks, kd = jax.random.split(key, 5)
        x = jax.random.normal(kx, (N, IN_DIM), dtype=jnp.float32) * 0.1
        adj_matrix = (jax.random.uniform(ka, (N, N)) < DENSITY).astype(jnp.float32)
        adj_matrix = jnp.maximum(adj_matrix, jnp.eye(N, dtype=jnp.float32))
        weight = jax.random.normal(kw, (OUT_DIM, IN_DIM), dtype=jnp.float32) * 0.05
        att_src = jax.random.normal(ks, (1, OUT_DIM), dtype=jnp.float32) * 0.1
        att_dst = jax.random.normal(kd, (1, OUT_DIM), dtype=jnp.float32) * 0.1
        return {'x': x, 'adj_matrix': adj_matrix, 'weight': weight, 'att_src': att_src, 'att_dst': att_dst}
    _L1_gnn_all = _L1_gnn_setup()
    _L1_gnn_in = {k: v for k, v in _L1_gnn_all.items() if k in ('weight', 'att_src', 'att_dst', )}
    del _L1_gnn_all

    def _L2_gnn_setup():
        import jax, jax.numpy as jnp
        import numpy as np
        N = 1024
        D = 128
        H = 8
        key = jax.random.key(seed)
        ks = jax.random.split(key, 7)
        s = (D * H) ** (-0.5)
        return {'x': jax.random.normal(ks[0], (N, D), dtype=jnp.float32), 'spatial_encoding': jax.random.normal(ks[1], (N, N), dtype=jnp.float32), 'edge_encoding': jax.random.normal(ks[2], (N, N), dtype=jnp.float32), 'Wq': jax.random.normal(ks[3], (D * H, D), dtype=jnp.float32) * s, 'Wk': jax.random.normal(ks[4], (D * H, D), dtype=jnp.float32) * s, 'Wv': jax.random.normal(ks[5], (D * H, D), dtype=jnp.float32) * s, 'Wo': jax.random.normal(ks[6], (D, D * H), dtype=jnp.float32) * s}
    _L2_gnn_all = _L2_gnn_setup()
    _L2_gnn_in = {k: v for k, v in _L2_gnn_all.items() if k in ('Wq', 'Wk', 'Wv', 'Wo', )}
    del _L2_gnn_all

    def _L3_gnn_setup():
        import jax, jax.numpy as jnp
        import numpy as np
        N = 8192
        IN_DIM = 128
        OUT_DIM = 128
        EDGE_P = 0.002
        key = jax.random.key(seed)
        k1, k2, k3, k4 = jax.random.split(key, 4)
        H = jax.random.normal(k1, (N, IN_DIM), dtype=jnp.float32)
        A = (jax.random.uniform(k2, (N, N)) < EDGE_P).astype(jnp.float32)
        limit = np.sqrt(6.0 / (IN_DIM + OUT_DIM)).astype(np.float32)
        W = jax.random.uniform(k3, (OUT_DIM, IN_DIM), minval=-limit, maxval=limit, dtype=jnp.float32)
        bound = 1.0 / np.sqrt(IN_DIM)
        b = jax.random.uniform(k4, (OUT_DIM,), minval=-bound, maxval=bound, dtype=jnp.float32)
        return {'H': H, 'A': A, 'W': W, 'b': b}
    _L3_gnn_all = _L3_gnn_setup()
    _L3_gnn_in = {k: v for k, v in _L3_gnn_all.items() if k in ('W', 'b', )}
    del _L3_gnn_all

    return {
        "x": x,
        "adj": adj,
        "L0_gnn_W": _L0_gnn_in["W"],
        "L0_gnn_b": _L0_gnn_in["b"],
        "L1_gnn_weight": _L1_gnn_in["weight"],
        "L1_gnn_att_src": _L1_gnn_in["att_src"],
        "L1_gnn_att_dst": _L1_gnn_in["att_dst"],
        "L2_gnn_Wq": _L2_gnn_in["Wq"],
        "L2_gnn_Wk": _L2_gnn_in["Wk"],
        "L2_gnn_Wv": _L2_gnn_in["Wv"],
        "L2_gnn_Wo": _L2_gnn_in["Wo"],
        "L3_gnn_W": _L3_gnn_in["W"],
        "L3_gnn_b": _L3_gnn_in["b"],
    }

def reference(x, adj, L0_gnn_W, L0_gnn_b, L1_gnn_weight, L1_gnn_att_src, L1_gnn_att_dst, L2_gnn_Wq, L2_gnn_Wk, L2_gnn_Wv, L2_gnn_Wo, L3_gnn_W, L3_gnn_b):
    import jax
    import jax.numpy as jnp
    def _L0_gnn_ref(x, adj, W, b):
        import jax, jax.numpy as jnp
        import numpy as np
        N = 8192
        F = 128
        U = 128
        EDGE_P = 0.002

        def adj_norm(adj):
            a_hat = adj + jnp.eye(adj.shape[0], dtype=adj.dtype)
            d_inv_sqrt = jax.lax.rsqrt(jnp.sum(a_hat, axis=-1))
            return a_hat * d_inv_sqrt[:, None] * d_inv_sqrt[None, :]
        adj_n = adj_norm(adj)
        h = adj_n @ x
        h = h @ W + b
        return jax.nn.relu(h)

    def _L1_gnn_ref(x, adj_matrix, weight, att_src, att_dst):
        import jax, jax.numpy as jnp
        import numpy as np
        N = 8192
        IN_DIM = 128
        OUT_DIM = 128
        DENSITY = 0.01
        H = x @ weight.T
        alpha_src = jnp.sum(H * att_src[0], axis=-1)
        alpha_dst = jnp.sum(H * att_dst[0], axis=-1)
        C = alpha_src[None, :] + alpha_dst[:, None]
        Tau = adj_matrix.T * jnp.exp(jnp.maximum(0.2 * C, C))
        att_weights = Tau / jnp.sum(Tau, axis=1, keepdims=True)
        Z = adj_matrix.T * att_weights @ H
        return Z

    def _L2_gnn_ref(x, spatial_encoding, edge_encoding, Wq, Wk, Wv, Wo):
        import jax, jax.numpy as jnp
        import numpy as np
        N = 1024
        D = 128
        H = 8
        n, d = x.shape
        h = Wq.shape[0] // d
        scale = d ** (-0.5)
        q = (x @ Wq.T).reshape(d, n, h)
        k = (x @ Wk.T).reshape(d, n, h)
        v = (x @ Wv.T).reshape(d, n, h)
        a = jnp.einsum('dnh,dmh->dnm', q, k) * scale
        a = a + spatial_encoding + edge_encoding
        a = jax.nn.softmax(a, axis=2)
        out = jnp.einsum('dnm,dmh->dnh', a, v)
        out = out.reshape(n, h * d)
        return out @ Wo.T

    def _L3_gnn_ref(H, A, W, b):
        import jax, jax.numpy as jnp
        import numpy as np
        N = 8192
        IN_DIM = 128
        OUT_DIM = 128
        EDGE_P = 0.002
        n = A.shape[0]
        A_t = A + jnp.eye(n, dtype=A.dtype)
        D = A_t.sum(axis=1)
        D_inv = jnp.where(D > 0, D ** (-0.5), jnp.zeros_like(D))
        A_norm = D_inv[:, None] * A_t * D_inv[None, :]
        HW = H @ W.T + b
        return jax.nn.relu(A_norm @ HW)

    x = _layernorm(x + _L0_gnn_ref(x, adj, L0_gnn_W, L0_gnn_b), axis=-1)
    x = _layernorm(x + _L1_gnn_ref(x, adj, L1_gnn_weight, L1_gnn_att_src, L1_gnn_att_dst), axis=-1)
    x = _layernorm(x + _L2_gnn_ref(x, adj, adj, L2_gnn_Wq, L2_gnn_Wk, L2_gnn_Wv, L2_gnn_Wo), axis=-1)
    x = _layernorm(x + _L3_gnn_ref(x, adj, L3_gnn_W, L3_gnn_b), axis=-1)
    return x


_drawn_inputs = setup_inputs


def setup_inputs(seed=0):
    import zlib

    import numpy as np

    out = dict(_drawn_inputs(seed))
    spreads = {'L0_gnn_b': (0.0, 0.1)}
    factors = {'L1_gnn_att_dst': 2.721,
     'L2_gnn_Wq': 8.0,
     'L2_gnn_Wk': 8.0,
     'L2_gnn_Wv': 6.718,
     'L2_gnn_Wo': 6.66}
    for name, (base, spread) in spreads.items():
        noise = np.random.default_rng([zlib.crc32(name.encode()), seed]).standard_normal(out[name].shape)
        drawn = base * np.exp(spread * noise) if base else spread * noise
        out[name] = jnp.asarray(drawn.astype(out[name].dtype))
    for name, factor in factors.items():
        out[name] = (out[name] * factor).astype(out[name].dtype)
    return out
```

```python
from contextlib import ExitStack

import concourse.bass as bass
from concourse import mybir

F32 = mybir.dt.float32
BF16 = mybir.dt.bfloat16
ALU = mybir.AluOpType
ACT = mybir.ActivationFunctionType
AX = mybir.AxisListType

P = 128
N = 2708
T = (N + P - 1) // P
NPAD = T * P
TAIL = N - (T - 1) * P
HEADS = 128
HD = 8
R = HEADS * N
EPS = 1e-5
LOWEST = -3.4028234663852886e38

BT = 4
FULL = T // BT
NB = FULL + 1
BW = BT * P
CW = 452
NC = 6
HALF = N // 2
HC = 3


def rows_of(t):
    return P if t < T - 1 else TAIL


def tiles_of(b):
    return BT if b < FULL else T - BT * FULL


def chunk(c):
    return min(CW, N - c * CW)


def program(nc, x, adj, w0, b0, w1, att_src, att_dst, wq, wk, wv, wo, w3, b3, ident_in, out):
    ctx = ExitStack()
    with ctx:
        def sb(name, shape, dt=F32):
            return ctx.enter_context(nc.sbuf_tensor(name, shape, dt))

        def sem(name):
            return ctx.enter_context(nc.semaphore(name))

        q_parts = nc.dram_tensor("q_parts", (HD * 3, R), BF16, kind="Internal").ap()
        k_parts = nc.dram_tensor("k_parts", (3 * HD, R), BF16, kind="Internal").ap()
        V_EXTRA = (124 * T - N) * HD
        v_flat = nc.dram_tensor("v_flat", (1, R * HD + V_EXTRA), F32, kind="Internal").ap()
        att_out = nc.dram_tensor("att_out", (4 * (HD + 1), R), F32, kind="Internal").ap()

        big = sb("big", [P, 2, BT, N])
        xn = sb("xn", [P, T, P])
        Z_AT, XT_AT = 0, NPAD
        W_AT = 2 * NPAD
        GS_AT = W_AT + 3 * HD * P
        WORK_AT = GS_AT + 2 * BW
        mem = sb("mem", [P, WORK_AT + 3 * NPAD])
        z = mem[:, Z_AT:XT_AT].rearrange("p (t f) -> p t f", f=P)
        xT = mem[:, XT_AT:W_AT]
        wqT, wkT, wvT = (mem[:, W_AT + i * HD * P:W_AT + (i + 1) * HD * P] for i in range(3))
        gs = mem[:, GS_AT:WORK_AT].rearrange("p (j n) -> p j n", j=2)
        work = mem[:, WORK_AT:WORK_AT + 3 * NPAD]
        ROWS_END = BT * N
        adj_rows = mem[:, 0:ROWS_END].rearrange("p (t n) -> p t n", t=BT)
        woR = sb("woR", [P, HD, P])
        w0s = sb("w0s", [P, P])
        w1T = sb("w1T", [P, P])
        w3T = sb("w3T", [P, P])
        b0r = sb("b0r", [P, P])
        b3r = sb("b3r", [P, P])
        ident = sb("ident", [P, P])
        ones = sb("ones", [P, P])
        dst_rep = sb("dst_rep", [P, P])
        asrc = sb("asrc", [P, 1])
        adst = sb("adst", [P, 1])
        ring = sb("ring", [P, 4 * 1360])
        rowsum = sb("rowsum", [P, T])
        dinv = sb("dinv", [P, T])
        dinv3 = sb("dinv3", [P, T])
        stat = sb("stat", [P, 6, T])
        as_col = sb("as_col", [P, 2, T])
        part_max = sb("part_max", [P, 2, BT, NC])
        neg_max = sb("neg_max", [P, 2, BT])

        psS = ctx.enter_context(nc.psum_tensor("psS", [P, 4, 512], F32))
        psP = ctx.enter_context(nc.psum_tensor("psP", [P, 3, 512], F32))
        psO = ctx.enter_context(nc.psum_tensor("psO", [P, 512], F32))

        aT = ring[:, 0:4 * BW].rearrange("p (r n) -> p r n", r=4)
        gat_e = ring[:, :].rearrange("p (r n) -> p r n", r=4)
        probs = ring[:, 0:4 * 1024].rearrange("p (r c n) -> p r c n", r=4, c=2)
        hT = work[:, 0:NPAD]
        adst_rows = work[:, NPAD:2 * NPAD]
        hn = work[:, 2 * NPAD:3 * NPAD].rearrange("p (t f) -> p t f", f=P)
        K_AT = ROWS_END
        Q_AT = K_AT + N
        VR_AT = Q_AT + 512
        kbuf = [mem[:, K_AT + j * (N // 2):K_AT + (j + 1) * (N // 2)].bitcast(BF16) for j in range(2)]
        qbuf = [mem[:, Q_AT + j * 256:Q_AT + (j + 1) * 256].bitcast(BF16) for j in range(2)]
        vraw = [mem[:, VR_AT + j * T * HD:VR_AT + (j + 1) * T * HD].rearrange("p (t h) -> p t h", h=HD)
                for j in range(2)]
        VP_AT = VR_AT + 2 * T * HD
        vpad_all = mem[:, VP_AT:VP_AT + 2 * T * 32]
        vpad = [mem[:, VP_AT + j * T * 32:VP_AT + (j + 1) * T * 32].rearrange("p (t c) -> p t c", c=32)
                for j in range(2)]
        OT_AT = VP_AT + 2 * T * 32
        obuf = [mem[:, OT_AT + j * BW:OT_AT + (j + 1) * BW] for j in range(2)]
        assert OT_AT + 2 * BW <= WORK_AT + 3 * NPAD
        wraw = work[:, 0:3 * 1024].rearrange("p (w t f) -> p w t f", w=3, t=HD)
        wo_raw = work[:, 3072:4096]
        w1_raw = work[:, 4096:4224]
        w3_raw = work[:, 4224:4352]
        bigf = big[:, :, :, :].rearrange("p j t n -> p (j t n)")
        scaled = [bigf[:, i * 1024:(i + 1) * 1024] for i in range(2)]
        rest = [bigf[:, (2 + i) * 1024:(3 + i) * 1024] for i in range(2)]
        v_out = [bigf[:, (4 + i) * 1024:(5 + i) * 1024] for i in range(2)]
        parts = [bigf[:, 6144 + i * 1536:6144 + (i + 1) * 1536].bitcast(BF16).rearrange("p (a n) -> p a n", a=3)
                 for i in range(4)]
        zero_row = bigf[0:1, 6144 + 4 * 1536:6144 + 4 * 1536 + V_EXTRA]
        G9 = 4 * (HD + 1) * P
        fin = [bigf[:, i * G9:(i + 1) * G9].rearrange("p (g h c) -> p g h c", g=4, c=P) for i in range(2)]
        mix = [bigf[:, 2 * G9 + i * 1024:2 * G9 + (i + 1) * 1024].rearrange("p (h c) -> p h c", c=P) for i in range(2)]
        mixT = [bigf[:, 2 * G9 + 2048 + i * 1024:2 * G9 + 3072 + i * 1024].rearrange("p (h c) -> p h c", c=P)
                for i in range(2)]
        rden = [bigf[:, 2 * G9 + 4096 + i * P:2 * G9 + 4096 + (i + 1) * P] for i in range(2)]

        in_small, in_x, in_w = sem("in_small"), sem("in_x"), sem("in_w")
        cleared = sem("cleared")
        w_turned, w_kept = sem("w_turned"), sem("w_kept")
        rs_in = [sem(f"rs_in{j}") for j in range(2)]
        rs_done = sem("rs_done")
        deg = sem("deg")
        gp = {}
        for L in (0, 3):
            gp[L] = dict(adj=[sem(f"g{L}_adj_in{j}") for j in range(2)], y=sem(f"g{L}_y_ready"),
                         tr=sem(f"g{L}_turned"), act=sem(f"g{L}_kept_by_act"), dve=sem(f"g{L}_kept_by_dve"),
                         mm=sem(f"g{L}_chunk_done"), g=sem(f"g{L}_product_ready"), gs=sem(f"g{L}_product_kept"),
                         out=sem(f"g{L}_tile_out"), z=sem(f"g{L}_tile_taken"))
        ln_z, ln_step, ln_var, ln_std, ln_x = sem("ln_z"), sem("ln_step"), sem("ln_var"), sem("ln_std"), sem("ln_x")
        xt_turned, xt_kept = sem("xt_turned"), sem("xt_kept")
        dst_ready = sem("dst_ready")
        h_made, h_kept = sem("h_made"), sem("h_kept")
        ad_made, ad_kept = sem("ad_made"), sem("ad_kept")
        hn_made, hn_kept = sem("hn_made"), sem("hn_kept")
        as_made, as_kept = sem("as_made"), sem("as_kept")
        gat_in = [sem(f"gat_adj_in{j}") for j in range(2)]
        e_ready, gat_w, gat_mm, gat_div, gat_rcp = (sem("e_ready"), sem("gat_weighted"), sem("gat_summed"),
                                                    sem("gat_divided"), sem("gat_reciprocal"))
        gz_turned, gz_added = sem("gz_turned"), sem("gz_added")
        pj_made, pj_act, pj_dve, pj_taken = sem("pj_made"), sem("pj_act"), sem("pj_dve"), sem("pj_v_kept")
        pj_zero = sem("pj_zero")
        pj_out = [sem(f"pj_out{j}") for j in range(2)]
        pj_tail = sem("pj_tail")
        at_clear = sem("at_clear")
        adj_in = sem("adj_in")
        kq_in = [sem(f"kq_in{j}") for j in range(2)]
        v_in = [sem(f"v_in{j}") for j in range(2)]
        v_padded = sem("v_padded")
        scored, taken = sem("scored"), sem("taken")
        max_part, max_ready = sem("max_part"), sem("max_ready")
        sub_pool, sub_act, sub_dve = sem("sub_pool"), sem("sub_act"), sem("sub_dve")
        turned, exp_done, pv_rounds = sem("turned"), sem("exp_done"), sem("pv_rounds")
        o_kept = sem("o_kept")
        o_out = [sem(f"o_out{j}") for j in range(2)]
        f_in = [sem(f"f_in{j}") for j in range(2)]
        f_half, f_step, f_mixed = sem("f_half"), sem("f_step"), sem("f_mixed")
        f_turned, f_kept, f_made, f_added = sem("f_turned"), sem("f_kept"), sem("f_made"), sem("f_added")
        y3_made, y3_biased = sem("y3_made"), sem("y3_biased")
        stored = sem("stored")
        passed = sem("passed")

        block = ctx.enter_context(nc.Block())

        UNITS = T // 2
        ROUNDS = (T + 3) // 4
        P1 = BT * NC

        class Head:
            def __init__(self, b, last):
                self.b, self.last = b, last
                self.nt = tiles_of(FULL) if last else BT
                self.w = N - FULL * BW if last else BW
                self.units = self.nt * NC

            def rows(self, t):
                return TAIL if self.last and t == self.nt - 1 else P

            def it(self, i):
                return self.b * HEADS + i

            def scored(self, i):
                return self.b * (HEADS * P1) + i * self.units + 1

            def maxes(self, i):
                return self.b * (HEADS * BT) + i * self.nt

            def subs_act(self, i):
                return self.b * (HEADS * 4) + i * (2 if self.last else 4)

            def turn(self, k):
                return self.b * (HEADS // 2) + k

        def settle(eng):
            eng.sem_inc(passed, 1)

        def act_pieces(h):
            return [(0, 0), (0, 1)] if h.last else [(1, 0), (1, 1), (2, 0), (2, 1)]

        def pipeline(eng, prologue, body):
            def one_block(h):
                prologue(h)
                with eng.Fori(0, HEADS // 2 - 1) as k:
                    for j in range(2):
                        body(h, k, j, True)
                body(h, HEADS // 2 - 1, 0, True)
                body(h, HEADS // 2 - 1, 1, False)
            with eng.Fori(0, FULL) as b:
                one_block(Head(b, False))
            one_block(Head(FULL, True))

        def z_or_y(L):
            return xT.rearrange("p (t f) -> p t f", f=P)

        def w_jobs():
            jobs = []
            for w, dst in enumerate((wqT, wkT, wvT)):
                jobs += [(wraw[:, w, t, :], dst[:, t * P:(t + 1) * P]) for t in range(HD)]
            wo_v = wo_raw.rearrange("o (c h) -> o h c", h=HD)
            jobs += [(wo_v[:, hh, :], woR[:, hh, :]) for hh in range(HD)]
            jobs += [(w1_raw, w1T[:, :]), (w3_raw, w3T[:, :])]
            return jobs

        @block.sync
        def _(sp):
            def load_adj(b, s, c0=0, c1=N):
                j = b % 2
                if b < FULL:
                    src = adj[b * BW:(b + 1) * BW, c0:c1].rearrange("(t p) c -> p t c", p=P)
                    sp.dma_start(big[:, j, 0:2, 0:c1 - c0], src[:, 0:2, :]).then_inc(s[j], 16)
                    sp.dma_start(big[:, j, 2:4, 0:c1 - c0], src[:, 2:4, :]).then_inc(s[j], 16)
                else:
                    r0 = FULL * BW
                    sp.dma_start(big[:, j, 0, 0:c1 - c0], adj[r0:r0 + P, c0:c1]).then_inc(s[j], 16)
                    sp.dma_start(big[0:TAIL, j, 1, 0:c1 - c0], adj[r0 + P:N, c0:c1]).then_inc(s[j], 16)

            sp.dma_start(ident[:, :], ident_in).then_inc(in_small, 16)
            sp.wait_ge(cleared, 2)
            load_adj(0, rs_in)
            load_adj(1, rs_in)
            for w, src in enumerate((wq, wk, wv)):
                sp.dma_start(wraw[:, w, :, :], src.rearrange("(t p) f -> p t f", p=P)).then_inc(in_w, 16)
            sp.dma_start(wo_raw, wo).then_inc(in_w, 16)
            sp.dma_start(w1_raw, w1).then_inc(in_w, 16)
            sp.dma_start(w3_raw, w3).then_inc(in_w, 16)
            sp.dma_start(w0s[:, :], w0).then_inc(in_small, 16)
            sp.dma_start(b0r[:, :], b0.rearrange("(a f) -> a f", a=1).broadcast_to([P, P])).then_inc(in_small, 16)
            sp.dma_start(b3r[:, :], b3.rearrange("(a f) -> a f", a=1).broadcast_to([P, P])).then_inc(in_small, 16)
            sp.dma_start(asrc[:, :], att_src.rearrange("a f -> f a")).then_inc(in_small, 16)
            sp.dma_start(adst[:, :], att_dst.rearrange("a f -> f a")).then_inc(in_small, 16)
            sp.dma_start(xn[:, 0:T - 1, :], x[0:(T - 1) * P, :].rearrange("(t p) f -> p t f", p=P)).then_inc(in_x, 16)
            sp.dma_start(xn[0:TAIL, T - 1, :], x[(T - 1) * P:N, :]).then_inc(in_x, 16)
            for b in range(2, NB):
                sp.wait_ge(rs_done, BT * (b - 1))
                load_adj(b, rs_in)

            for b in range(NB):
                if b < 2:
                    sp.wait_ge(rs_done, T if b == 1 else BT * (NB - 1))
                else:
                    sp.wait_ge(gp[0]["tr"], T * (b - 1))
                load_adj(b, gp[0]["adj"])

            for s in range(2 * NB):
                half, b = divmod(s, NB)
                if s < 2:
                    sp.wait_ge(gp[0]["tr"], T * (NB - 1 + b))
                else:
                    done = sum(tiles_of(u % NB) for u in range(s - 1))
                    sp.wait_ge(gat_w, 3 * done)
                load_adj(b, gat_in, half * HALF, (half + 1) * HALF)

            sp.wait_ge(pj_zero, 1)
            sp.dma_start(v_flat[0:1, R * HD:R * HD + V_EXTRA], zero_row).then_inc(pj_tail, 16)
            for t in range(T):
                r, j = rows_of(t), t % 2
                at = t * P * P
                for which, dst in ((0, q_parts), (1, k_parts)):
                    sp.wait_ge(pj_dve, 4 * t + 2 * which + 2)
                    for a in range(3):
                        src = parts[2 * j + which][0:r, a, :].rearrange("p (h c) -> p h c", c=P)
                        view = dst.rearrange("(h a) r -> h a r", a=3)[:, a] if which == 0 else \
                            dst.rearrange("(a h) r -> a h r", a=3)[a]
                        view = view[:, at:at + r * P].rearrange("h (p c) -> p h c", c=P)
                        sp.dma_start(view, src).then_inc(pj_out[j], 16)
                sp.wait_ge(pj_taken, t + 1)
                sp.dma_start(v_flat[0, t * P * 1024:(t * P + r) * 1024].rearrange("(p n) -> p n", n=1024),
                             v_out[j][0:r, :]).then_inc(pj_out[j], 16)
            for j in range(2):
                sp.wait_ge(pj_out[j], 7 * 16 * (T // 2))
            sp.wait_ge(pj_tail, 16)
            sp.wait_ge(at_clear, 3)

            def load_head(h, i, j):
                row0 = i * N
                for a in range(3):
                    sp.dma_start(qbuf[j][24 * a:24 * a + 24, 0:h.w],
                                 q_parts[:, bass.ds(row0 + h.b * BW, h.w)]).then_inc(kq_in[j], 16)
                    sp.dma_start(kbuf[j][a:72:3, :], k_parts[:, bass.ds(row0, N)]).then_inc(kq_in[j], 16)
                sp.dma_start(vraw[j][0:124, :, :],
                             v_flat[0, bass.ds(i * (N * HD), 124 * T * HD)]
                             .rearrange("(p t h) -> p t h", t=T, h=HD)).then_inc(v_in[j], 16)

            def load_block(h):
                sp.wait_ge(taken, h.scored(0) + 3)
                settle(sp)
                for t in range(h.nt):
                    r = h.rows(t)
                    sp.dma_start(adj_rows[0:r, t, :], adj[bass.ds(h.b * BW + t * P, r), :]).then_inc(adj_in, 16)
                sp.wait_ge(scored, h.scored(0))
                settle(sp)
                sp.wait_ge(v_padded, h.it(0) + 1)
                settle(sp)
                load_head(h, 0, 0)
                load_head(h, 1, 1)

            def step(h, k, j, has_next):
                i = 2 * k + j
                if not (isinstance(k, int)):
                    sp.wait_ge(scored, h.scored(i + 1))
                    settle(sp)
                    sp.wait_ge(v_padded, h.it(i) + 2)
                    settle(sp)
                    load_head(h, i + 2, j)
                sp.wait_ge(o_kept, h.it(i) + 2)
                settle(sp)
                for g in range(4):
                    sp.dma_start(att_out[(HD + 1) * g:(HD + 1) * (g + 1), bass.ds(i * N + h.b * BW, h.w)],
                                 obuf[j][32 * g:32 * g + HD + 1, 0:h.w]).then_inc(o_out[j], 16)

            pipeline(sp, load_block, step)

            for j in range(2):
                sp.wait_ge(o_out[j], 64 * NB * (HEADS // 2) + 1)
            for t in range(T):
                r, j = rows_of(t), t % 2
                if t >= 2:
                    sp.wait_ge(f_mixed, t - 1)
                for g in range(4):
                    src = att_out[(HD + 1) * g:(HD + 1) * (g + 1), t * P * P:(t * P + r) * P]
                    sp.dma_start(fin[j][0:r, g, :, :], src.rearrange("h (p c) -> p h c", c=P)).then_inc(f_in[j], 16)
            for b in range(NB):
                if b < 2:
                    sp.wait_ge(f_made, T)
                else:
                    sp.wait_ge(gp[3]["tr"], T * (b - 1))
                load_adj(b, gp[3]["adj"])
            sp.wait_ge(ln_x, 4)
            sp.dma_start(out[0:(T - 1) * P, :].rearrange("(t p) f -> p t f", p=P), xn[:, 0:T - 1, :]).then_inc(stored, 16)
            sp.dma_start(out[(T - 1) * P:N, :], xn[0:TAIL, T - 1, :]).then_inc(stored, 16)
            sp.wait_ge(stored, 32)

        @block.tensor
        def _(pe):
            pe.wait_ge(in_small, 96)
            pe.wait_ge(in_w, 96)
            for n, (src, _) in enumerate(w_jobs()):
                if n >= 4:
                    pe.wait_ge(w_kept, n - 3)
                pe.transpose(psS[:, n % 4, 0:P], src, ident[:, :]).then_inc(w_turned, 1)

            def product(L, first_bank_free):
                g = gp[L]
                pe.wait_ge(g["y"], 1)
                for s, v in first_bank_free:
                    pe.wait_ge(s, v)

                def chunk_mm(b, c):
                    gc, w = b * T + c, tiles_of(b) * P
                    pe.wait_ge(g["act"] if gc % 2 == 0 else g["dve"], gc // 2 + 1)
                    if c == 0 and b > 0:
                        pe.wait_ge(g["gs"], b)
                    r = rows_of(c)
                    pe.matmul(psO[:, 0:w], z_or_y(L)[0:r, c, :], aT[0:r, gc % 4, 0:w], start=(c == 0), stop=False,
                              skip_group_check=True).then_inc(g["mm"], 1)

                for b in range(NB):
                    nt = tiles_of(b)
                    pe.wait_ge(g["adj"][b % 2], 32 * (b // 2 + 1))
                    for c in range(T):
                        gc = b * T + c
                        if gc >= 4:
                            pe.wait_ge(g["act"] if gc % 2 == 0 else g["dve"], (gc - 4) // 2 + 1)
                        for t in range(nt):
                            r = rows_of(c)
                            mm = pe.transpose(psS[0:r, gc % 4, t * P:(t + 1) * P],
                                              big[:, b % 2, t, c * P:c * P + r], ident[:, :])
                        mm.then_inc(g["tr"], 1)
                        if c >= 2:
                            chunk_mm(b, c - 2)
                    chunk_mm(b, T - 2)
                    chunk_mm(b, T - 1)
                    for t in range(nt):
                        r = rows_of(BT * b + t)
                        mm = pe.matmul(psO[:, t * P:t * P + r], z_or_y(L)[0:r, BT * b + t, :], ident[0:r, 0:r],
                                       start=False, stop=(t == nt - 1), skip_group_check=True)
                    mm.then_inc(g["g"], 1)
                    pe.wait_ge(g["gs"], b + 1)
                    for t in range(nt):
                        n = BT * b + t
                        if n >= 3:
                            pe.wait_ge(g["z"], n - 2)
                        lhs = gs[:, b % 2, t * P:(t + 1) * P]
                        if L == 0:
                            mm = pe.matmul(psP[:, n % 3, 0:P], lhs, w0s[:, :], start=True, stop=True)
                        else:
                            mm = pe.transpose(psP[:, n % 3, 0:P], lhs, ident[:, :])
                        mm.then_inc(g["out"], 1)

            def turn_features(n):
                pe.wait_ge(ln_x, n + 1)
                for q in range(NB):
                    if q >= 4 or n > 0:
                        pe.wait_ge(xt_kept, n * NB + max(q - 3, 0))
                    for t in range(tiles_of(q)):
                        mm = pe.transpose(psS[:, q % 4, t * P:(t + 1) * P], xn[:, BT * q + t, :], ident[:, :])
                    mm.then_inc(xt_turned, 1)

            product(0, [(w_kept, len(w_jobs()))])

            turn_features(0)
            pe.wait_ge(xt_kept, NB)
            for q in range(NB):
                w = tiles_of(q) * P
                if q >= 3:
                    pe.wait_ge(h_kept, q - 2)
                pe.matmul(psP[:, q % 3, 0:w], w1T[:, :], xT[:, q * BW:q * BW + w], start=True, stop=True)\
                    .then_inc(h_made, 1)
            pe.wait_ge(dst_ready, 1)
            pe.wait_ge(h_kept, NB)
            for q in range(NB):
                w = tiles_of(q) * P
                if q >= 3:
                    pe.wait_ge(ad_kept, q - 2)
                pe.matmul(psP[:, q % 3, 0:w], dst_rep[:, :], hT[:, q * BW:q * BW + w], start=True, stop=True)\
                    .then_inc(ad_made, 1)
            for q in range(NB):
                if q >= 4:
                    pe.wait_ge(hn_kept, q - 3)
                for t in range(tiles_of(q)):
                    mm = pe.transpose(psS[:, q % 4, t * P:(t + 1) * P],
                                      hT[:, (BT * q + t) * P:(BT * q + t + 1) * P], ident[:, :])
                mm.then_inc(hn_made, 1)
            for t in range(T):
                mm = pe.matmul(psO[:, t:t + 1], hT[:, t * P:(t + 1) * P], asrc[:, :], start=True, stop=True,
                               skip_group_check=True)
            mm.then_inc(as_made, 1)
            pe.wait_ge(hn_kept, NB)
            pe.wait_ge(ad_kept, NB)
            for s in range(2 * T):
                half, t = divmod(s, T)
                r = rows_of(t)
                if t == 0 and half:
                    pe.wait_ge(gat_div, HC)
                for kind in range(2):
                    pe.wait_ge(gat_w, 3 * s + 2 + kind)
                    for c in range(HC):
                        w = min(CW, HALF - c * CW)
                        mm = pe.matmul((psS if kind == 0 else psP)[:, c, 0:w],
                                       ones[0:r, :] if kind == 0 else hn[0:r, t, :],
                                       gat_e[0:r, 2 * (s % 2) + kind, c * CW:c * CW + w],
                                       start=(t == 0), stop=(t == T - 1), skip_group_check=True)
                mm.then_inc(gat_mm, 1)
            pe.wait_ge(gat_div, 2 * HC)
            for q in range(NB):
                if q >= 4:
                    pe.wait_ge(gz_added, q - 3)
                for t in range(tiles_of(q)):
                    mm = pe.transpose(psS[:, q % 4, t * P:(t + 1) * P],
                                      xT[:, (BT * q + t) * P:(BT * q + t + 1) * P], ident[:, :])
                mm.then_inc(gz_turned, 1)

            turn_features(1)
            pe.wait_ge(xt_kept, 2 * NB)
            for n in range(3 * T):
                t, which = divmod(n, 3)
                if t:
                    pe.wait_ge(*((pj_taken, t) if which == 2 else (pj_act, 6 * (t - 1) + 3 * which + 2)))
                bank = (psS[:, 0:2], psS[:, 2:4], psP[:, 0:2])[which]
                for c in range(2):
                    mm = pe.matmul(bank[:, c, :], xT[:, t * P:(t + 1) * P],
                                   (wqT, wkT, wvT)[which][:, c * 512:(c + 1) * 512], start=True, stop=True)
                mm.then_inc(pj_made, 1)
            pe.wait_ge(pj_act, 6 * T)
            pe.wait_ge(pj_taken, T)
            pe.wait_ge(at_clear, 3)

            def score(h, i, j, q):
                t, c = divmod(q, NC)
                pe.wait_ge(taken, h.scored(i) + q + 1)
                r, w = h.rows(t), chunk(c)
                pe.matmul(psP[0:r, q % 3, 0:w], qbuf[j][0:96, t * P:t * P + r], kbuf[j][0:96, c * CW:c * CW + w],
                          start=True, stop=True).then_inc(scored, 1)

            def first_scores(h):
                pe.wait_ge(kq_in[0], 96 * h.turn(0) + 96)
                for q in range(h.units):
                    score(h, 0, 0, q)

            def values(h, i, j, rnd):
                if rnd == 0:
                    pe.wait_ge(v_padded, h.it(i) + 2)
                    pe.wait_ge(o_kept, h.it(i) + 1)
                pe.wait_ge(exp_done, UNITS * h.it(i) + min(2 * rnd + 2, UNITS) + 1)
                for c in range(4 * rnd, min(4 * rnd + 4, T)):
                    r = 124 if c < 2 else 123
                    g = c % 4
                    mm = pe.matmul(psO[32 * g:32 * g + 32, 0:h.w], vpad[j][0:r, c, :],
                                   probs[0:r, c // 2 % 4, c % 2, 0:h.w], start=(c < 4), stop=(c + 4 >= T),
                                   skip_group_check=True)
                mm.then_inc(pv_rounds, 1)

            def step(h, k, j, has_next):
                i, jn = 2 * k + j, 1 - j
                if not h.last:
                    pe.wait_ge(sub_pool, h.it(i) + 1)
                pe.wait_ge(sub_act, h.subs_act(i + 1))
                pe.wait_ge(sub_dve, h.it(i) + 1)
                q = 0
                for u in range(UNITS):
                    if u == 0:
                        pe.wait_ge(exp_done, UNITS * h.it(i) + 1)
                        if has_next:
                            pe.wait_ge(kq_in[jn], 96 * h.turn(k + j) + 96)
                    elif u >= 2:
                        pe.wait_ge(exp_done, UNITS * h.it(i) + u)
                    r = 124 if u == 0 else 123
                    for c in range(2):
                        for t in range(h.nt):
                            m = h.rows(t)
                            first = 2 * u + c
                            mm = pe.transpose(psS[0:r, u % 2 * 2 + c, t * P:t * P + m],
                                              big[0:m, j, t, first:first + T * (r - 1) + 1:T], ident[0:m, 0:m])
                    mm.then_inc(turned, 1)
                    if has_next:
                        until = min(h.units, (u + 1) * h.units // 8)
                        while q < until:
                            score(h, i + 1, jn, q)
                            q += 1
                    if u >= 3 and u % 2:
                        values(h, i, j, (u - 3) // 2)
                values(h, i, j, ROUNDS - 2)
                values(h, i, j, ROUNDS - 1)

            pipeline(pe, first_scores, step)

            pe.wait_ge(o_kept, NB * HEADS + 1)
            for t in range(T):
                if t >= 2:
                    pe.wait_ge(f_kept, 2 * (t - 1))
                pe.wait_ge(f_mixed, t + 1)
                for hh in range(HD):
                    mm = pe.transpose(psS[:, 2 * (t % 2) + hh // 4, hh % 4 * P:hh % 4 * P + P], mix[t % 2][:, hh, :],
                                      ident[:, :])
                mm.then_inc(f_turned, 1)
                pe.wait_ge(f_kept, 2 * t + 2)
                if t >= 3:
                    pe.wait_ge(f_added, t - 2)
                for hh in range(HD):
                    mm = pe.matmul(psP[:, t % 3, 0:P], mixT[t % 2][:, hh, :], woR[:, hh, :], start=(hh == 0),
                                   stop=(hh == HD - 1))
                mm.then_inc(f_made, 1)

            turn_features(2)
            pe.wait_ge(xt_kept, 3 * NB)
            pe.wait_ge(f_added, T)
            for t in range(T):
                if t >= 3:
                    pe.wait_ge(y3_biased, t - 2)
                pe.matmul(psP[:, t % 3, 0:P], xT[:, t * P:(t + 1) * P], w3T[:, :], start=True, stop=True)\
                    .then_inc(y3_made, 1)
            product(3, [])

        @block.scalar
        def _(act):
            for n, (_, dst) in enumerate(w_jobs()):
                act.wait_ge(w_turned, n + 1)
                act.activation(dst, psS[:, n % 4, 0:P], ACT.Copy).then_inc(w_kept, 1)
            act.wait_ge(deg, 1)
            act.activation(stat[:, 1, :], stat[:, 0, :], ACT.Sqrt).then_inc(deg, 1)

            def product(L):
                g = gp[L]
                for b in range(NB):
                    w = tiles_of(b) * P
                    for c in range(0, T, 2):
                        gc = b * T + c
                        act.wait_ge(g["tr"], gc + 1)
                        if gc >= 4:
                            act.wait_ge(g["mm"], gc - 3)
                        act.activation(aT[:, gc % 4, 0:w], psS[:, gc % 4, 0:w], ACT.Copy).then_inc(g["act"], 1)
                    act.wait_ge(g["g"], b + 1)
                    if b >= 2:
                        act.wait_ge(g["out"], BT * (b - 1))
                    act.activation(gs[:, b % 2, 0:w], psO[:, 0:w], ACT.Copy).then_inc(g["gs"], 1)

            def norm(n):
                act.wait_ge(ln_var, n + 1)
                act.activation(stat[:, 3, :], stat[:, 2, :], ACT.Sqrt).then_inc(ln_std, 1)

            def keep_features(n):
                for q in range(NB):
                    w = tiles_of(q) * P
                    act.wait_ge(xt_turned, n * NB + q + 1)
                    act.activation(xT[:, q * BW:q * BW + w], psS[:, q % 4, 0:w], ACT.Copy).then_inc(xt_kept, 1)

            product(0)
            norm(0)
            keep_features(0)
            for made, kept, dst in ((h_made, h_kept, hT), (ad_made, ad_kept, adst_rows)):
                for q in range(NB):
                    w = tiles_of(q) * P
                    act.wait_ge(made, q + 1)
                    act.activation(dst[:, q * BW:q * BW + w], psP[:, q % 3, 0:w], ACT.Copy).then_inc(kept, 1)
            act.wait_ge(as_made, 1)
            act.activation(as_col[:, 0, :], psO[:, 0:T], ACT.Copy).then_inc(as_kept, 1)
            act.activation(as_col[:, 1, :], psO[:, 0:T], ACT.Copy, scale=0.2).then_inc(as_kept, 1)
            act.wait_ge(as_kept, 2)
            act.wait_ge(ad_kept, NB)
            for s in range(2 * T):
                half, t = divmod(s, T)
                if s >= 2:
                    act.wait_ge(gat_mm, s - 1)
                cols = adst_rows[:, half * HALF:(half + 1) * HALF]
                act.activation(gat_e[:, 2 * (s % 2), 0:HALF], cols, ACT.Exp, bias=as_col[:, 0, t:t + 1])\
                    .then_inc(e_ready, 1)
                act.activation(gat_e[:, 2 * (s % 2) + 1, 0:HALF], cols, ACT.Exp, bias=as_col[:, 1, t:t + 1],
                               scale=0.2).then_inc(e_ready, 1)
            norm(1)
            keep_features(1)
            for t in range(T):
                j = t % 2
                for which in range(2):
                    act.wait_ge(pj_made, 3 * t + which + 1)
                    src = psS[:, 2 * which:2 * which + 2, :].rearrange("p a (c h) -> p h a c", h=HD)
                    scale = 0.5 * float(P) ** -0.5 if which == 0 else 1.0
                    if t:
                        act.wait_ge(pj_dve, 4 * (t - 1) + 2 * which + 2)
                    if t >= 2:
                        act.wait_ge(pj_out[j], 7 * 16 * (t // 2))
                    act.activation(scaled[which].rearrange("p (h a c) -> p h a c", h=HD, a=2), src, ACT.Copy,
                                   scale=scale).then_inc(pj_act, 1)
                    act.activation(parts[2 * j + which][:, 0, :].rearrange("p (h a c) -> p h a c", h=HD, a=2), src,
                                   ACT.Copy, scale=scale).then_inc(pj_act, 1)
                    act.wait_ge(pj_dve, 4 * t + 2 * which + 1)
                    act.activation(parts[2 * j + which][:, 1, :], rest[which], ACT.Copy).then_inc(pj_act, 1)

            def subtract(h, i, j, piece):
                t, half = act_pieces(h)[piece]
                if half == 0:
                    act.wait_ge(max_ready, h.maxes(i) + t + 1)
                r = h.rows(t)
                part = big[0:r, j, t, half * HALF:(half + 1) * HALF]
                act.activation(part, part, ACT.Identity, bias=neg_max[0:r, j, t:t + 1]).then_inc(sub_act, 1)

            def first_subtract(h):
                for piece in range(len(act_pieces(h))):
                    subtract(h, 0, 0, piece)

            def step(h, k, j, has_next):
                i = 2 * k + j
                at = {8: 0, 9: 1} if h.last else {5: 0, 6: 1, 8: 2, 9: 3}
                for u in range(UNITS):
                    r = 124 if u == 0 else 123
                    act.wait_ge(turned, UNITS * h.it(i) + u + 2)
                    if u in (0, 2) or u >= 4:
                        rounds = {0: ROUNDS - 1, 2: ROUNDS}.get(u, ROUNDS + (u - 4) // 2 + 1)
                        act.wait_ge(pv_rounds, ROUNDS * h.it(i) + rounds)
                    act.activation(probs[0:r, u % 4, :, 0:h.w], psS[0:r, u % 2 * 2:u % 2 * 2 + 2, 0:h.w], ACT.Exp,
                                   scale=2.0).then_inc(exp_done, 1)
                    if has_next and u in at:
                        subtract(h, i + 1, 1 - j, at[u])
                act.wait_ge(pv_rounds, ROUNDS * h.it(i) + 2 * ROUNDS)
                act.wait_ge(o_out[j], 64 * h.turn(k) + 1)
                act.activation(obuf[j][:, 0:h.w], psO[:, 0:h.w], ACT.Copy).then_inc(o_kept, 1)

            pipeline(act, first_subtract, step)

            for t in range(T):
                act.wait_ge(f_turned, t + 1)
                if t >= 2:
                    act.wait_ge(f_made, t - 1)
                for a in range(2):
                    act.activation(mixT[t % 2][:, 4 * a:4 * a + 4, :].rearrange("p h c -> p (h c)"),
                                   psS[:, 2 * (t % 2) + a, :], ACT.Copy).then_inc(f_kept, 1)
            norm(2)
            keep_features(2)
            product(3)
            norm(3)

        @block.gpsimd
        def _(pool):
            pool.memset(ones[:, :], 1.0).then_inc(cleared, 1)
            pool.memset(xn[:, T - 1, :], 0.0).then_inc(cleared, 1)
            pool.wait_ge(gat_div, 2 * HC)
            pool.memset(mem[64:96, K_AT:VR_AT], 0.0).then_inc(at_clear, 1)
            pool.wait_ge(at_clear, 1)
            pool.memset(vpad_all, 0.0).then_inc(at_clear, 1)
            pool.wait_ge(at_clear, 2)
            pool.memset(vpad_all.rearrange("p (t c) -> p t c", c=32)[:, :, HD:HD + 1], 1.0).then_inc(at_clear, 1)
            pool.wait_ge(at_clear, 3)

            def pad_values(h, i, k, j):
                pool.wait_ge(v_in[j], 16 * h.turn(k) + 16)
                settle(pool)
                pool.tensor_copy(vpad[j][0:124, :, 0:HD], vraw[j][0:124, :, :]).then_inc(v_padded, 1)

            def subtract(h, i, j):
                pool.wait_ge(max_ready, h.maxes(i) + 1)
                part = big[:, j, 0, 0:N]
                pool.tensor_tensor(part, part, neg_max[:, j, 0:1].broadcast_to([P, N]), ALU.add)\
                    .then_inc(sub_pool, 1)

            def first(h):
                pool.wait_ge(pv_rounds, ROUNDS * h.it(0) + ROUNDS)
                pad_values(h, 0, 0, 0)
                if not h.last:
                    subtract(h, 0, 0)

            def step(h, k, j, has_next):
                i, jn = 2 * k + j, 1 - j
                if has_next:
                    pool.wait_ge(pv_rounds, ROUNDS * h.it(i) + ROUNDS)
                    pad_values(h, i + 1, k + j, jn)
                    if not h.last:
                        subtract(h, i + 1, jn)

            pipeline(pool, first, step)

        @block.vector
        def _(dve):
            for b in range(NB):
                dve.wait_ge(rs_in[b % 2], 32 * (b // 2 + 1))
                for t in range(tiles_of(b)):
                    dve.tensor_reduce(rowsum[:, BT * b + t:BT * b + t + 1], big[:, b % 2, t, 0:N], AX.X, ALU.add)\
                        .then_inc(rs_done, 1)
            dve.wait_ge(rs_done, T)
            steps = [0]

            def chained(ins):
                steps[0] += 1
                ins.then_inc(ln_step, 1)
                dve.wait_ge(ln_step, steps[0])

            chained(dve.tensor_scalar(rowsum[:, :], rowsum[:, :], 1.0, None, ALU.add))
            dve.tensor_scalar(stat[:, 0, :], rowsum[:, :], 1e-30, None, ALU.max).then_inc(deg, 1)
            dve.wait_ge(deg, 2)
            chained(dve.reciprocal(dinv[:, :], stat[:, 1, :]))
            chained(dve.tensor_scalar(stat[:, 4, :], rowsum[:, :], 0.0, None, ALU.is_gt))
            chained(dve.tensor_tensor(dinv3[:, :], dinv[:, :], stat[:, 4, :], ALU.mult))

            def by_node(ap):
                return ap.unsqueeze(2).broadcast_to([P, T, P])

            def product(L):
                g = gp[L]
                for b in range(NB):
                    w = tiles_of(b) * P
                    for c in range(1, T, 2):
                        gc = b * T + c
                        dve.wait_ge(g["tr"], gc + 1)
                        if gc >= 4:
                            dve.wait_ge(g["mm"], gc - 3)
                        dve.tensor_copy(aT[:, gc % 4, 0:w], psS[:, gc % 4, 0:w]).then_inc(g["dve"], 1)
                    for t in range(tiles_of(b)):
                        n = BT * b + t
                        dve.wait_ge(g["out"], n + 1)
                        if L == 0:
                            ins = dve.scalar_tensor_tensor(out=z[:, n, :], in0=psP[:, n % 3, 0:P],
                                                           scalar=dinv[:, n:n + 1], in1=b0r[:, :],
                                                           op0=ALU.mult, op1=ALU.add)
                        else:
                            ins = dve.tensor_scalar(z[:, n, :], psP[:, n % 3, 0:P], dinv3[:, n:n + 1], None, ALU.mult)
                        ins.then_inc(g["z"], 1)
                dve.wait_ge(g["z"], T)
                chained(dve.scalar_tensor_tensor(out=z[:, :, :], in0=z[:, :, :], scalar=0.0, in1=xn[:, :, :],
                                                 op0=ALU.max, op1=ALU.add))

            def norm(n):
                chained(dve.tensor_reduce(stat[:, 0, :], z[:, :, :], AX.X, ALU.add))
                chained(dve.tensor_scalar(stat[:, 1, :], stat[:, 0, :], 1.0 / P, None, ALU.mult))
                chained(dve.tensor_tensor(z[:, :, :], z[:, :, :], by_node(stat[:, 1, :]), ALU.subtract))
                chained(dve.tensor_tensor(xn[:, :, :], z[:, :, :], z[:, :, :], ALU.mult))
                chained(dve.tensor_reduce(stat[:, 0, :], xn[:, :, :], AX.X, ALU.add))
                dve.tensor_scalar(stat[:, 2, :], stat[:, 0, :], 1.0 / P, EPS, ALU.mult, ALU.add).then_inc(ln_var, 1)
                dve.wait_ge(ln_std, n + 1)
                chained(dve.reciprocal(stat[:, 5, :], stat[:, 3, :]))
                dve.tensor_tensor(xn[:, :, :], z[:, :, :], by_node(stat[:, 5, :]), ALU.mult).then_inc(ln_x, 1)

            dve.wait_ge(in_x, 32)
            dve.wait_ge(in_small, 96)
            dve.wait_ge(cleared, 2)
            dve.tensor_tensor(z_or_y(0), xn[:, :, :], by_node(dinv[:, :]), ALU.mult).then_inc(gp[0]["y"], 1)
            product(0)
            norm(0)

            dve.tensor_scalar(dst_rep[:, :], ones[:, :], adst[:, 0:1], None, ALU.mult).then_inc(dst_ready, 1)
            for q in range(NB):
                w = tiles_of(q)
                dve.wait_ge(hn_made, q + 1)
                dve.tensor_copy(hn[:, BT * q:BT * q + w, :].rearrange("p t f -> p (t f)"), psS[:, q % 4, 0:w * P])\
                    .then_inc(hn_kept, 1)
            made = 0
            loads = 0
            for s in range(2 * T):
                half, t = divmod(s, T)
                b, tb = divmod(t, BT)
                slot = b % 2
                if tb == 0:
                    dve.wait_ge(gat_in[slot], 32 * (half * (NB // 2) + b // 2 + 1))
                e1, e2 = gat_e[:, 2 * (s % 2), 0:HALF], gat_e[:, 2 * (s % 2) + 1, 0:HALF]
                rows = big[:, slot, tb, 0:HALF]
                dve.wait_ge(e_ready, 2 * s + 2)
                dve.tensor_tensor(e1, e1, e2, ALU.max).then_inc(gat_w, 1)
                dve.wait_ge(gat_w, 3 * s + 1)
                dve.tensor_tensor(e1, e1, rows, ALU.mult).then_inc(gat_w, 1)
                dve.wait_ge(gat_w, 3 * s + 2)
                dve.tensor_tensor(e2, e1, rows, ALU.mult).then_inc(gat_w, 1)
                if t == T - 1:
                    dve.wait_ge(gat_mm, s + 1)
                    rec = z[:, :, :].rearrange("p t f -> p (t f)")
                    for c in range(HC):
                        w = min(CW, HALF - c * CW)
                        dve.reciprocal(rec[:, c * CW:c * CW + w], psS[:, c, 0:w]).then_inc(gat_rcp, 1)
                    for c in range(HC):
                        w = min(CW, HALF - c * CW)
                        dve.wait_ge(gat_rcp, HC * half + c + 1)
                        dve.tensor_tensor(xT[:, half * HALF + c * CW:half * HALF + c * CW + w], psP[:, c, 0:w],
                                          rec[:, c * CW:c * CW + w], ALU.mult).then_inc(gat_div, 1)
            for q in range(NB):
                w = tiles_of(q)
                dve.wait_ge(gz_turned, q + 1)
                dve.tensor_tensor(z[:, BT * q:BT * q + w, :], psS[:, q % 4, 0:w * P].rearrange("p (t f) -> p t f", f=P),
                                  xn[:, BT * q:BT * q + w, :], ALU.add).then_inc(gz_added, 1)
            dve.wait_ge(gz_added, NB)
            norm(1)

            dve.memset(zero_row, 0.0).then_inc(pj_zero, 1)
            for t in range(T):
                j = t % 2
                for which in range(2):
                    part = parts[2 * j + which]
                    dve.wait_ge(pj_act, 6 * t + 3 * which + 2)
                    dve.tensor_tensor(rest[which], scaled[which], part[:, 0, :], ALU.subtract).then_inc(pj_dve, 1)
                    dve.wait_ge(pj_act, 6 * t + 3 * which + 3)
                    dve.wait_ge(pj_dve, 4 * t + 2 * which + 1)
                    dve.tensor_tensor(part[:, 2, :], rest[which], part[:, 1, :], ALU.subtract).then_inc(pj_dve, 1)
                dve.wait_ge(pj_made, 3 * t + 3)
                if t >= 2:
                    dve.wait_ge(pj_out[j], 7 * 16 * (t // 2))
                ins = dve.tensor_copy(v_out[j].rearrange("p (a n) -> p a n", a=2), psP[:, 0:2, :])
                ins.then_inc(pj_taken, 1)
            for j in range(2):
                dve.wait_ge(pj_out[j], 7 * 16 * (T // 2))
            dve.wait_ge(pj_tail, 16)
            dve.sem_inc(taken, 4)
            for s in (scored, exp_done, o_kept, turned, v_padded, *o_out):
                dve.sem_inc(s, 1)
            dve.sem_inc(pv_rounds, ROUNDS)

            def score_max(h, i, j):
                units = h.units
                for q in range(units + 1):
                    if q < units:
                        t, c = divmod(q, NC)
                        r, w = h.rows(t), chunk(c)
                        dve.wait_ge(scored, h.scored(i) + q + 1)
                        settle(dve)
                        dve.tensor_tensor_reduce(big[0:r, j, t, c * CW:c * CW + w], psP[0:r, q % 3, 0:w],
                                                 adj_rows[0:r, t, c * CW:c * CW + w], 1.0, LOWEST, ALU.add, ALU.max,
                                                 part_max[0:r, j, t, c:c + 1]).then_inc(taken, 1)
                    if q and q % NC == 0:
                        t = q // NC - 1
                        r = h.rows(t)
                        dve.wait_ge(taken, h.scored(i) + q + 3)
                        dve.tensor_reduce(neg_max[0:r, j, t:t + 1], part_max[0:r, j, t, :], AX.X, ALU.max,
                                          negate=True).then_inc(max_ready, 1)
                t = h.nt - 1
                r = h.rows(t)
                dve.wait_ge(max_ready, h.maxes(i) + h.nt)
                part = big[0:r, j, t, 0:N]
                dve.tensor_scalar(part, part, neg_max[0:r, j, t:t + 1], None, ALU.add).then_inc(sub_dve, 1)

            def first_scores(h):
                dve.wait_ge(adj_in, 64 * (h.b + 1) if not h.last else 64 * FULL + 32)
                dve.wait_ge(turned, UNITS * h.it(0) + 1)
                score_max(h, 0, 0)

            def step(h, k, j, has_next):
                i = 2 * k + j
                if has_next:
                    dve.wait_ge(turned, UNITS * h.it(i) + 1)
                    score_max(h, i + 1, 1 - j)

            pipeline(dve, first_scores, step)

            for t in range(T):
                j = t % 2
                if t < 2:
                    dve.wait_ge(turned, UNITS * NB * HEADS + 1)
                dve.wait_ge(f_in[j], 64 * (t // 2 + 1))
                f = [fin[j][:, g, :, :] for g in range(4)]
                chained(dve.tensor_tensor(f[0], f[0], f[1], ALU.add))
                chained(dve.tensor_tensor(f[2], f[2], f[3], ALU.add))
                chained(dve.tensor_tensor(f[0], f[0], f[2], ALU.add))
                chained(dve.reciprocal(rden[j], fin[j][:, 0, HD, :]))
                if t >= 2:
                    dve.wait_ge(f_turned, t - 1)
                dve.tensor_tensor(mix[j], fin[j][:, 0, 0:HD, :], rden[j].unsqueeze(1).broadcast_to([P, HD, P]),
                                  ALU.mult).then_inc(f_mixed, 1)
                if t:
                    dve.wait_ge(f_made, t)
                    dve.tensor_tensor(z[:, t - 1, :], psP[:, (t - 1) % 3, 0:P], xn[:, t - 1, :], ALU.add)\
                        .then_inc(f_added, 1)
            dve.wait_ge(f_made, T)
            dve.tensor_tensor(z[:, T - 1, :], psP[:, (T - 1) % 3, 0:P], xn[:, T - 1, :], ALU.add).then_inc(f_added, 1)
            dve.wait_ge(f_added, T)
            norm(2)

            y3 = z_or_y(3)
            for t in range(T):
                dve.wait_ge(y3_made, t + 1)
                dve.tensor_tensor(z[:, t, :], psP[:, t % 3, 0:P], b3r[:, :], ALU.add).then_inc(y3_biased, 1)
            dve.wait_ge(y3_biased, T)
            dve.tensor_tensor(y3, z[:, :, :], by_node(dinv3[:, :]), ALU.mult).then_inc(gp[3]["y"], 1)
            product(3)
            norm(3)


_INS = ["x", "adj", "L0_gnn_W", "L0_gnn_b", "L1_gnn_weight", "L1_gnn_att_src", "L1_gnn_att_dst", "L2_gnn_Wq",
        "L2_gnn_Wk", "L2_gnn_Wv", "L2_gnn_Wo", "L3_gnn_W", "L3_gnn_b"]


def kernel(**inputs):
    import numpy as _np
    import concourse.bacc as _bacc
    from concourse import mybir as _mybir
    from concourse.bass_utils import run_bass_kernel_spmd as _run

    nc = _bacc.Bacc("TRN2", target_bir_lowering=False, num_devices=1)
    arrays, args = {}, []
    for name in _INS:
        a = _np.ascontiguousarray(inputs[name])
        arrays[f"in_{name}"] = a
        args.append(nc.dram_tensor(f"in_{name}", a.shape, _mybir.dt.from_np(a.dtype), kind="ExternalInput").ap())
    arrays["identity"] = _np.eye(P, dtype=_np.float32)
    args.append(nc.dram_tensor("identity", (P, P), F32, kind="ExternalInput").ap())
    out = nc.dram_tensor("out_0", (N, P), F32, kind="ExternalOutput").ap()
    program(nc, *args, out)
    r = _run(nc, [arrays], core_ids=[0])
    return r.results[0]["out_0"]
```

```python
from contextlib import ExitStack

import concourse.bass as bass
from concourse import mybir

F32 = mybir.dt.float32
BF16 = mybir.dt.bfloat16
ALU = mybir.AluOpType
ACT = mybir.ActivationFunctionType
AX = mybir.AxisListType

P = 128
N = 2708
T = (N + P - 1) // P
NPAD = T * P
TAIL = N - (T - 1) * P
HEADS = 128
HD = 8
R = HEADS * N
EPS = 1e-5
LOWEST = -3.4028234663852886e38

BT = 4
FULL = T // BT
NB = FULL + 1
BW = BT * P
CW = 452
NC = 6
HALF = N // 2
HC = 3


def rows_of(t):
    return P if t < T - 1 else TAIL


def tiles_of(b):
    return BT if b < FULL else T - BT * FULL


def chunk(c):
    return min(CW, N - c * CW)


def program(nc, x, adj, w0, b0, w1, att_src, att_dst, wq, wk, wv, wo, w3, b3, ident_in, out):
    ctx = ExitStack()
    with ctx:
        def sb(name, shape, dt=F32):
            return ctx.enter_context(nc.sbuf_tensor(name, shape, dt))

        def sem(name):
            return ctx.enter_context(nc.semaphore(name))

        q_parts = nc.dram_tensor("q_parts", (HD * 3, R), BF16, kind="Internal").ap()
        k_parts = nc.dram_tensor("k_parts", (3 * HD, R), BF16, kind="Internal").ap()
        V_EXTRA = (124 * T - N) * HD
        v_flat = nc.dram_tensor("v_flat", (1, R * HD + V_EXTRA), F32, kind="Internal").ap()
        att_out = nc.dram_tensor("att_out", (4 * (HD + 1), R), F32, kind="Internal").ap()

        big = sb("big", [P, 2, BT, N])
        xn = sb("xn", [P, T, P])
        Z_AT, XT_AT = 0, NPAD
        W_AT = 2 * NPAD
        GS_AT = W_AT + 3 * HD * P
        WORK_AT = GS_AT + 2 * BW
        mem = sb("mem", [P, WORK_AT + 3 * NPAD])
        z = mem[:, Z_AT:XT_AT].rearrange("p (t f) -> p t f", f=P)
        xT = mem[:, XT_AT:W_AT]
        wqT, wkT, wvT = (mem[:, W_AT + i * HD * P:W_AT + (i + 1) * HD * P] for i in range(3))
        gs = mem[:, GS_AT:WORK_AT].rearrange("p (j n) -> p j n", j=2)
        work = mem[:, WORK_AT:WORK_AT + 3 * NPAD]
        ROWS_END = BT * N
        adj_rows = mem[:, 0:ROWS_END].rearrange("p (t n) -> p t n", t=BT)
        woR = sb("woR", [P, HD, P])
        w0s = sb("w0s", [P, P])
        w1T = sb("w1T", [P, P])
        w3T = sb("w3T", [P, P])
        b0r = sb("b0r", [P, P])
        b3r = sb("b3r", [P, P])
        ident = sb("ident", [P, P])
        ones = sb("ones", [P, P])
        dst_rep = sb("dst_rep", [P, P])
        asrc = sb("asrc", [P, 1])
        adst = sb("adst", [P, 1])
        RING = 6
        ring = sb("ring", [P, RING * 1024])
        rowsum = sb("rowsum", [P, T])
        dinv = sb("dinv", [P, T])
        dinv3 = sb("dinv3", [P, T])
        stat = sb("stat", [P, 6, T])
        as_col = sb("as_col", [P, 2, T])
        part_max = sb("part_max", [P, 2, BT, NC])
        neg_max = sb("neg_max", [P, 2, BT])

        psS = ctx.enter_context(nc.psum_tensor("psS", [P, 4, 512], F32))
        psP = ctx.enter_context(nc.psum_tensor("psP", [P, 3, 512], F32))
        psO = ctx.enter_context(nc.psum_tensor("psO", [P, 512], F32))

        aT = ring[:, 0:4 * BW].rearrange("p (r n) -> p r n", r=4)
        gat_e = ring[:, 0:4 * HALF].rearrange("p (r n) -> p r n", r=4)
        probs = ring[:, :].rearrange("p (r c n) -> p r c n", r=RING, c=2)
        hT = work[:, 0:NPAD]
        adst_rows = work[:, NPAD:2 * NPAD]
        hn = work[:, 2 * NPAD:3 * NPAD].rearrange("p (t f) -> p t f", f=P)
        K_AT = ROWS_END
        Q_AT = K_AT + N
        VR_AT = Q_AT + 512
        kbuf = [mem[:, K_AT + j * (N // 2):K_AT + (j + 1) * (N // 2)].bitcast(BF16) for j in range(2)]
        qbuf = [mem[:, Q_AT + j * 256:Q_AT + (j + 1) * 256].bitcast(BF16) for j in range(2)]
        vraw = [mem[:, VR_AT + j * T * HD:VR_AT + (j + 1) * T * HD].rearrange("p (t h) -> p t h", h=HD)
                for j in range(2)]
        VP_AT = VR_AT + 2 * T * HD
        vpad_all = mem[:, VP_AT:VP_AT + 2 * T * 32]
        vpad = [mem[:, VP_AT + j * T * 32:VP_AT + (j + 1) * T * 32].rearrange("p (t c) -> p t c", c=32)
                for j in range(2)]
        OT_AT = VP_AT + 2 * T * 32
        obuf = [mem[:, OT_AT + j * BW:OT_AT + (j + 1) * BW] for j in range(2)]
        assert OT_AT + 2 * BW <= WORK_AT + 3 * NPAD
        wraw = work[:, 0:3 * 1024].rearrange("p (w t f) -> p w t f", w=3, t=HD)
        wo_raw = work[:, 3072:4096]
        w1_raw = work[:, 4096:4224]
        w3_raw = work[:, 4224:4352]
        bigf = big[:, :, :, :].rearrange("p j t n -> p (j t n)")
        scaled = [bigf[:, i * 1024:(i + 1) * 1024] for i in range(2)]
        rest = [bigf[:, (2 + i) * 1024:(3 + i) * 1024] for i in range(2)]
        v_out = [bigf[:, (4 + i) * 1024:(5 + i) * 1024] for i in range(2)]
        parts = [bigf[:, 6144 + i * 1536:6144 + (i + 1) * 1536].bitcast(BF16).rearrange("p (a n) -> p a n", a=3)
                 for i in range(4)]
        zero_row = bigf[0:1, 6144 + 4 * 1536:6144 + 4 * 1536 + V_EXTRA]
        G9 = 4 * (HD + 1) * P
        fin = [bigf[:, i * G9:(i + 1) * G9].rearrange("p (g h c) -> p g h c", g=4, c=P) for i in range(2)]
        mix = [bigf[:, 2 * G9 + i * 1024:2 * G9 + (i + 1) * 1024].rearrange("p (h c) -> p h c", c=P) for i in range(2)]
        mixT = [bigf[:, 2 * G9 + 2048 + i * 1024:2 * G9 + 3072 + i * 1024].rearrange("p (h c) -> p h c", c=P)
                for i in range(2)]
        rden = [bigf[:, 2 * G9 + 4096 + i * P:2 * G9 + 4096 + (i + 1) * P] for i in range(2)]

        in_small, in_x, in_w = sem("in_small"), sem("in_x"), sem("in_w")
        cleared = sem("cleared")
        w_turned, w_kept = sem("w_turned"), sem("w_kept")
        rs_in = [sem(f"rs_in{j}") for j in range(2)]
        rs_done = sem("rs_done")
        deg = sem("deg")
        gp = {}
        for L in (0, 3):
            gp[L] = dict(adj=[sem(f"g{L}_adj_in{j}") for j in range(2)], y=sem(f"g{L}_y_ready"),
                         tr=sem(f"g{L}_turned"), act=sem(f"g{L}_kept_by_act"), dve=sem(f"g{L}_kept_by_dve"),
                         mm=sem(f"g{L}_chunk_done"), g=sem(f"g{L}_product_ready"), gs=sem(f"g{L}_product_kept"),
                         out=sem(f"g{L}_tile_out"), z=sem(f"g{L}_tile_taken"))
        ln_z, ln_step, ln_var, ln_std, ln_x = sem("ln_z"), sem("ln_step"), sem("ln_var"), sem("ln_std"), sem("ln_x")
        xt_turned, xt_kept = sem("xt_turned"), sem("xt_kept")
        dst_ready = sem("dst_ready")
        h_made, h_kept = sem("h_made"), sem("h_kept")
        ad_made, ad_kept = sem("ad_made"), sem("ad_kept")
        hn_made, hn_kept = sem("hn_made"), sem("hn_kept")
        as_made, as_kept = sem("as_made"), sem("as_kept")
        gat_in = [sem(f"gat_adj_in{j}") for j in range(2)]
        e_ready, gat_w, gat_mm, gat_div, gat_rcp = (sem("e_ready"), sem("gat_weighted"), sem("gat_summed"),
                                                    sem("gat_divided"), sem("gat_reciprocal"))
        gz_turned, gz_added = sem("gz_turned"), sem("gz_added")
        pj_made, pj_act, pj_dve, pj_taken = sem("pj_made"), sem("pj_act"), sem("pj_dve"), sem("pj_v_kept")
        pj_zero = sem("pj_zero")
        pj_out = [sem(f"pj_out{j}") for j in range(2)]
        pj_tail = sem("pj_tail")
        at_clear = sem("at_clear")
        adj_in = [sem(f"adj_in{t}") for t in range(BT)]
        kq_in = [sem(f"kq_in{j}") for j in range(2)]
        v_in = [sem(f"v_in{j}") for j in range(2)]
        v_padded = sem("v_padded")
        scored, taken = sem("scored"), sem("taken")
        max_part, max_ready = sem("max_part"), sem("max_ready")
        sub_pool, sub_act, sub_dve = sem("sub_pool"), sem("sub_act"), sem("sub_dve")
        turned, exp_done, pv_rounds = sem("turned"), sem("exp_done"), sem("pv_rounds")
        o_kept = sem("o_kept")
        o_out = [sem(f"o_out{j}") for j in range(2)]
        f_in = [sem(f"f_in{j}") for j in range(2)]
        f_half, f_step, f_mixed = sem("f_half"), sem("f_step"), sem("f_mixed")
        f_turned, f_kept, f_made, f_added = sem("f_turned"), sem("f_kept"), sem("f_made"), sem("f_added")
        y3_made, y3_biased = sem("y3_made"), sem("y3_biased")
        stored = sem("stored")
        passed = sem("passed")

        block = ctx.enter_context(nc.Block())

        UNITS = T // 2
        ROUNDS = (T + 3) // 4
        P1 = BT * NC

        PIECES = {"pool": [(0, 0), (0, 1), (1, 0), (2, 0)], "act": [(1, 1), (3, 0)], "dve": [(2, 1), (3, 1)]}
        LAST_PIECES = {"pool": [(0, 0)], "act": [(0, 1), (1, 0)], "dve": [(1, 1)]}

        class Head:
            def __init__(self, b, last):
                self.b, self.last = b, last
                self.nt = tiles_of(FULL) if last else BT
                self.w = N - FULL * BW if last else BW
                self.units = self.nt * NC
                self.early, self.spread = 3, 16 if last else 17

            def rows(self, t):
                return TAIL if self.last and t == self.nt - 1 else P

            def it(self, i):
                return self.b * HEADS + i

            def scored(self, i):
                return self.b * (HEADS * P1) + i * self.units + 1

            def maxes(self, i):
                return self.b * (HEADS * BT) + i * self.nt

            def subs(self, eng, i):
                return self.b * (HEADS * len(PIECES[eng])) + i * len(self.pieces(eng))

            def pieces(self, eng):
                return (LAST_PIECES if self.last else PIECES)[eng]

            def exps(self, i):
                return self.it(i) * UNITS + 2

            def turns(self, i):
                return self.it(i) * UNITS + UNITS + 1

            def turn(self, k):
                return self.b * (HEADS // 2) + k

        def settle(eng):
            eng.sem_inc(passed, 1)

        def pair(j, u):
            return 2 * ((u + j) % 2)

        def slot(j, u):
            return (u + j * (UNITS % RING)) % RING

        def slot_free(j, u):
            if u >= RING:
                return ROUNDS + (u - RING) // 2 + 1
            before = max(v for v in range(UNITS) if slot(1 - j, v) == slot(j, u))
            return before // 2 + 1

        def blocks_of_heads(eng, h, prologue, body, epilogue=None):
            prologue(h)
            body(h, 0, 0, True, True)
            body(h, 0, 1, False, True)
            with eng.Fori(1, HEADS // 2 - 1) as k:
                for j in range(2):
                    body(h, k, j, False, True)
            body(h, HEADS // 2 - 1, 0, False, True)
            body(h, HEADS // 2 - 1, 1, False, False)
            if epilogue:
                epilogue(h)

        def pipeline(eng, prologue, body, epilogue=None):
            full, last, pairs = Head(0, False), Head(FULL, True), FULL * HEADS // 2

            def two_heads(h, k, before, after):
                body(h, k, 0, before, (h, 2 * k + 1))
                body(h, k, 1, (h, 2 * k), after)

            prologue(full)
            two_heads(full, 0, None, (full, 2))
            with eng.Fori(1, pairs - 1) as k:
                two_heads(full, k, (full, 2 * k - 1), (full, 2 * k + 2))
            two_heads(full, pairs - 1, (full, 2 * pairs - 3), (last, 0))
            two_heads(last, 0, (full, 2 * pairs - 1), (last, 2))
            with eng.Fori(1, HEADS // 2 - 1) as k:
                two_heads(last, k, (last, 2 * k - 1), (last, 2 * k + 2))
            two_heads(last, HEADS // 2 - 1, (last, HEADS - 3), None)
            if epilogue:
                epilogue(last)

        def z_or_y(L):
            return xT.rearrange("p (t f) -> p t f", f=P)

        def w_jobs():
            jobs = []
            for w, dst in enumerate((wqT, wkT, wvT)):
                jobs += [(wraw[:, w, t, :], dst[:, t * P:(t + 1) * P]) for t in range(HD)]
            wo_v = wo_raw.rearrange("o (c h) -> o h c", h=HD)
            jobs += [(wo_v[:, hh, :], woR[:, hh, :]) for hh in range(HD)]
            jobs += [(w1_raw, w1T[:, :]), (w3_raw, w3T[:, :])]
            return jobs

        @block.sync
        def _(sp):
            def load_adj(b, s, c0=0, c1=N):
                j = b % 2
                if b < FULL:
                    src = adj[b * BW:(b + 1) * BW, c0:c1].rearrange("(t p) c -> p t c", p=P)
                    sp.dma_start(big[:, j, 0:2, 0:c1 - c0], src[:, 0:2, :]).then_inc(s[j], 16)
                    sp.dma_start(big[:, j, 2:4, 0:c1 - c0], src[:, 2:4, :]).then_inc(s[j], 16)
                else:
                    r0 = FULL * BW
                    sp.dma_start(big[:, j, 0, 0:c1 - c0], adj[r0:r0 + P, c0:c1]).then_inc(s[j], 16)
                    sp.dma_start(big[0:TAIL, j, 1, 0:c1 - c0], adj[r0 + P:N, c0:c1]).then_inc(s[j], 16)

            sp.dma_start(ident[:, :], ident_in).then_inc(in_small, 16)
            sp.wait_ge(cleared, 2)
            load_adj(0, rs_in)
            load_adj(1, rs_in)
            for w, src in enumerate((wq, wk, wv)):
                sp.dma_start(wraw[:, w, :, :], src.rearrange("(t p) f -> p t f", p=P)).then_inc(in_w, 16)
            sp.dma_start(wo_raw, wo).then_inc(in_w, 16)
            sp.dma_start(w1_raw, w1).then_inc(in_w, 16)
            sp.dma_start(w3_raw, w3).then_inc(in_w, 16)
            sp.dma_start(w0s[:, :], w0).then_inc(in_small, 16)
            sp.dma_start(b0r[:, :], b0.rearrange("(a f) -> a f", a=1).broadcast_to([P, P])).then_inc(in_small, 16)
            sp.dma_start(b3r[:, :], b3.rearrange("(a f) -> a f", a=1).broadcast_to([P, P])).then_inc(in_small, 16)
            sp.dma_start(asrc[:, :], att_src.rearrange("a f -> f a")).then_inc(in_small, 16)
            sp.dma_start(adst[:, :], att_dst.rearrange("a f -> f a")).then_inc(in_small, 16)
            sp.dma_start(xn[:, 0:T - 1, :], x[0:(T - 1) * P, :].rearrange("(t p) f -> p t f", p=P)).then_inc(in_x, 16)
            sp.dma_start(xn[0:TAIL, T - 1, :], x[(T - 1) * P:N, :]).then_inc(in_x, 16)
            for b in range(2, NB):
                sp.wait_ge(rs_done, BT * (b - 1))
                load_adj(b, rs_in)

            for b in range(NB):
                if b < 2:
                    sp.wait_ge(rs_done, T if b == 1 else BT * (NB - 1))
                else:
                    sp.wait_ge(gp[0]["tr"], T * (b - 1))
                load_adj(b, gp[0]["adj"])

            for s in range(2 * NB):
                half, b = divmod(s, NB)
                if s < 2:
                    sp.wait_ge(gp[0]["tr"], T * (NB - 1 + b))
                else:
                    done = sum(tiles_of(u % NB) for u in range(s - 1))
                    sp.wait_ge(gat_w, 3 * done)
                load_adj(b, gat_in, half * HALF, (half + 1) * HALF)

            sp.wait_ge(pj_zero, 1)
            sp.dma_start(v_flat[0:1, R * HD:R * HD + V_EXTRA], zero_row).then_inc(pj_tail, 16)
            for t in range(T):
                r, j = rows_of(t), t % 2
                at = t * P * P
                for which, dst in ((0, q_parts), (1, k_parts)):
                    sp.wait_ge(pj_dve, 4 * t + 2 * which + 2)
                    for a in range(3):
                        src = parts[2 * j + which][0:r, a, :].rearrange("p (h c) -> p h c", c=P)
                        view = dst.rearrange("(h a) r -> h a r", a=3)[:, a] if which == 0 else \
                            dst.rearrange("(a h) r -> a h r", a=3)[a]
                        view = view[:, at:at + r * P].rearrange("h (p c) -> p h c", c=P)
                        sp.dma_start(view, src).then_inc(pj_out[j], 16)
                sp.wait_ge(pj_taken, t + 1)
                sp.dma_start(v_flat[0, t * P * 1024:(t * P + r) * 1024].rearrange("(p n) -> p n", n=1024),
                             v_out[j][0:r, :]).then_inc(pj_out[j], 16)
            for j in range(2):
                sp.wait_ge(pj_out[j], 7 * 16 * (T // 2))
            sp.wait_ge(pj_tail, 16)
            sp.wait_ge(at_clear, 3)

            def load_head(h, i, j):
                row0 = i * N
                for a in range(3):
                    sp.dma_start(qbuf[j][24 * a:24 * a + 24, 0:h.w],
                                 q_parts[:, bass.ds(row0 + h.b * BW, h.w)]).then_inc(kq_in[j], 16)
                    sp.dma_start(kbuf[j][a:72:3, :], k_parts[:, bass.ds(row0, N)]).then_inc(kq_in[j], 16)
                sp.dma_start(vraw[j][0:124, :, :],
                             v_flat[0, bass.ds(i * (N * HD), 124 * T * HD)]
                             .rearrange("(p t h) -> p t h", t=T, h=HD)).then_inc(v_in[j], 16)

            def load_rows(h, before=None):
                for t in range(h.nt):
                    if before:
                        sp.wait_ge(taken, before.scored(HEADS - 1) + NC * (t + 1) + 3)
                        settle(sp)
                    r = h.rows(t)
                    sp.dma_start(adj_rows[0:r, t, :], adj[bass.ds(h.b * BW + t * P, r), :]).then_inc(adj_in[t], 16)

            def no_prologue(h):
                pass

            def store_sums(h, i, j):
                sp.wait_ge(o_kept, h.it(i) + 2)
                settle(sp)
                for g in range(4):
                    sp.dma_start(att_out[(HD + 1) * g:(HD + 1) * (g + 1), bass.ds(i * N + h.b * BW, h.w)],
                                 obuf[j][32 * g:32 * g + HD + 1, 0:h.w]).then_inc(o_out[j], 16)

            def last_store(h):
                store_sums(h, HEADS - 1, 1)

            def step_before(after):
                def step(h, k, j, first, has_next):
                    i = 2 * k + j
                    in_block = not (isinstance(k, int) and k == HEADS // 2 - 1)
                    if in_block or after:
                        sp.wait_ge(scored, h.scored(i + 1))
                        settle(sp)
                        sp.wait_ge(v_padded, h.it(i) + 2)
                        settle(sp)
                        if in_block:
                            load_head(h, i + 2, j)
                        else:
                            load_head(after(h), j, j)
                            if j == 0:
                                load_rows(after(h), h)
                    if not first:
                        store_sums(h, i - 1, 1 - j)
                return step

            load_head(Head(0, False), 0, 0)
            load_rows(Head(0, False))
            load_head(Head(0, False), 1, 1)
            with sp.Fori(0, FULL - 1) as b:
                blocks_of_heads(sp, Head(b, False), no_prologue, step_before(lambda h: Head(h.b + 1, False)),
                                last_store)
            blocks_of_heads(sp, Head(FULL - 1, False), no_prologue, step_before(lambda h: Head(FULL, True)),
                            last_store)
            blocks_of_heads(sp, Head(FULL, True), no_prologue, step_before(None), last_store)

            for j in range(2):
                sp.wait_ge(o_out[j], 64 * NB * (HEADS // 2) + 1)
            for t in range(T):
                r, j = rows_of(t), t % 2
                if t >= 2:
                    sp.wait_ge(f_mixed, t - 1)
                for g in range(4):
                    src = att_out[(HD + 1) * g:(HD + 1) * (g + 1), t * P * P:(t * P + r) * P]
                    sp.dma_start(fin[j][0:r, g, :, :], src.rearrange("h (p c) -> p h c", c=P)).then_inc(f_in[j], 16)
            for b in range(NB):
                if b < 2:
                    sp.wait_ge(f_made, T)
                else:
                    sp.wait_ge(gp[3]["tr"], T * (b - 1))
                load_adj(b, gp[3]["adj"])
            sp.wait_ge(ln_x, 4)
            sp.dma_start(out[0:(T - 1) * P, :].rearrange("(t p) f -> p t f", p=P), xn[:, 0:T - 1, :]).then_inc(stored, 16)
            sp.dma_start(out[(T - 1) * P:N, :], xn[0:TAIL, T - 1, :]).then_inc(stored, 16)
            sp.wait_ge(stored, 32)

        @block.tensor
        def _(pe):
            pe.wait_ge(in_small, 96)
            pe.wait_ge(in_w, 96)
            for n, (src, _) in enumerate(w_jobs()):
                if n >= 4:
                    pe.wait_ge(w_kept, n - 3)
                pe.transpose(psS[:, n % 4, 0:P], src, ident[:, :]).then_inc(w_turned, 1)

            def product(L, first_bank_free):
                g = gp[L]
                pe.wait_ge(g["y"], 1)
                for s, v in first_bank_free:
                    pe.wait_ge(s, v)

                def chunk_mm(b, c):
                    gc, w = b * T + c, tiles_of(b) * P
                    pe.wait_ge(g["act"] if gc % 2 == 0 else g["dve"], gc // 2 + 1)
                    if c == 0 and b > 0:
                        pe.wait_ge(g["gs"], b)
                    r = rows_of(c)
                    pe.matmul(psO[:, 0:w], z_or_y(L)[0:r, c, :], aT[0:r, gc % 4, 0:w], start=(c == 0), stop=False,
                              skip_group_check=True).then_inc(g["mm"], 1)

                for b in range(NB):
                    nt = tiles_of(b)
                    pe.wait_ge(g["adj"][b % 2], 32 * (b // 2 + 1))
                    for c in range(T):
                        gc = b * T + c
                        if gc >= 4:
                            pe.wait_ge(g["act"] if gc % 2 == 0 else g["dve"], (gc - 4) // 2 + 1)
                        for t in range(nt):
                            r = rows_of(c)
                            mm = pe.transpose(psS[0:r, gc % 4, t * P:(t + 1) * P],
                                              big[:, b % 2, t, c * P:c * P + r], ident[:, :])
                        mm.then_inc(g["tr"], 1)
                        if c >= 2:
                            chunk_mm(b, c - 2)
                    chunk_mm(b, T - 2)
                    chunk_mm(b, T - 1)
                    for t in range(nt):
                        r = rows_of(BT * b + t)
                        mm = pe.matmul(psO[:, t * P:t * P + r], z_or_y(L)[0:r, BT * b + t, :], ident[0:r, 0:r],
                                       start=False, stop=(t == nt - 1), skip_group_check=True)
                    mm.then_inc(g["g"], 1)
                    pe.wait_ge(g["gs"], b + 1)
                    for t in range(nt):
                        n = BT * b + t
                        if n >= 3:
                            pe.wait_ge(g["z"], n - 2)
                        lhs = gs[:, b % 2, t * P:(t + 1) * P]
                        if L == 0:
                            mm = pe.matmul(psP[:, n % 3, 0:P], lhs, w0s[:, :], start=True, stop=True)
                        else:
                            mm = pe.transpose(psP[:, n % 3, 0:P], lhs, ident[:, :])
                        mm.then_inc(g["out"], 1)

            def turn_features(n):
                pe.wait_ge(ln_x, n + 1)
                for q in range(NB):
                    if q >= 4 or n > 0:
                        pe.wait_ge(xt_kept, n * NB + max(q - 3, 0))
                    for t in range(tiles_of(q)):
                        mm = pe.transpose(psS[:, q % 4, t * P:(t + 1) * P], xn[:, BT * q + t, :], ident[:, :])
                    mm.then_inc(xt_turned, 1)

            product(0, [(w_kept, len(w_jobs()))])

            turn_features(0)
            pe.wait_ge(xt_kept, NB)
            for q in range(NB):
                w = tiles_of(q) * P
                if q >= 3:
                    pe.wait_ge(h_kept, q - 2)
                pe.matmul(psP[:, q % 3, 0:w], w1T[:, :], xT[:, q * BW:q * BW + w], start=True, stop=True)\
                    .then_inc(h_made, 1)
            pe.wait_ge(dst_ready, 1)
            pe.wait_ge(h_kept, NB)
            for q in range(NB):
                w = tiles_of(q) * P
                if q >= 3:
                    pe.wait_ge(ad_kept, q - 2)
                pe.matmul(psP[:, q % 3, 0:w], dst_rep[:, :], hT[:, q * BW:q * BW + w], start=True, stop=True)\
                    .then_inc(ad_made, 1)
            for q in range(NB):
                if q >= 4:
                    pe.wait_ge(hn_kept, q - 3)
                for t in range(tiles_of(q)):
                    mm = pe.transpose(psS[:, q % 4, t * P:(t + 1) * P],
                                      hT[:, (BT * q + t) * P:(BT * q + t + 1) * P], ident[:, :])
                mm.then_inc(hn_made, 1)
            for t in range(T):
                mm = pe.matmul(psO[:, t:t + 1], hT[:, t * P:(t + 1) * P], asrc[:, :], start=True, stop=True,
                               skip_group_check=True)
            mm.then_inc(as_made, 1)
            pe.wait_ge(hn_kept, NB)
            pe.wait_ge(ad_kept, NB)
            for s in range(2 * T):
                half, t = divmod(s, T)
                r = rows_of(t)
                if t == 0 and half:
                    pe.wait_ge(gat_div, HC)
                for kind in range(2):
                    pe.wait_ge(gat_w, 3 * s + 2 + kind)
                    for c in range(HC):
                        w = min(CW, HALF - c * CW)
                        mm = pe.matmul((psS if kind == 0 else psP)[:, c, 0:w],
                                       ones[0:r, :] if kind == 0 else hn[0:r, t, :],
                                       gat_e[0:r, 2 * (s % 2) + kind, c * CW:c * CW + w],
                                       start=(t == 0), stop=(t == T - 1), skip_group_check=True)
                mm.then_inc(gat_mm, 1)
            pe.wait_ge(gat_div, 2 * HC)
            for q in range(NB):
                if q >= 4:
                    pe.wait_ge(gz_added, q - 3)
                for t in range(tiles_of(q)):
                    mm = pe.transpose(psS[:, q % 4, t * P:(t + 1) * P],
                                      xT[:, (BT * q + t) * P:(BT * q + t + 1) * P], ident[:, :])
                mm.then_inc(gz_turned, 1)

            turn_features(1)
            pe.wait_ge(xt_kept, 2 * NB)
            for n in range(3 * T):
                t, which = divmod(n, 3)
                if t:
                    pe.wait_ge(*((pj_taken, t) if which == 2 else (pj_act, 6 * (t - 1) + 3 * which + 2)))
                bank = (psS[:, 0:2], psS[:, 2:4], psP[:, 0:2])[which]
                for c in range(2):
                    mm = pe.matmul(bank[:, c, :], xT[:, t * P:(t + 1) * P],
                                   (wqT, wkT, wvT)[which][:, c * 512:(c + 1) * 512], start=True, stop=True)
                mm.then_inc(pj_made, 1)
            pe.wait_ge(pj_act, 6 * T)
            pe.wait_ge(pj_taken, T)
            pe.wait_ge(at_clear, 3)

            def score(h, i, j, q):
                t, c = divmod(q, NC)
                pe.wait_ge(taken, h.scored(i) + q + 1)
                r, w = h.rows(t), chunk(c)
                pe.matmul(psP[0:r, q % 3, 0:w], qbuf[j][0:96, t * P:t * P + r], kbuf[j][0:96, c * CW:c * CW + w],
                          start=True, stop=True).then_inc(scored, 1)

            def first_scores(h):
                pe.wait_ge(kq_in[0], 96 * h.turn(0) + 96)
                for q in range(h.units):
                    score(h, 0, 0, q)

            def values(h, i, j, rnd):
                if rnd == 0:
                    pe.wait_ge(v_padded, h.it(i) + 2)
                    pe.wait_ge(o_kept, h.it(i) + 1)
                pe.wait_ge(exp_done, h.exps(i) + min(2 * rnd + 2, UNITS))
                last = rnd == ROUNDS - 1
                for g in range(4):
                    c = 4 * rnd + (g // 2 if last else g)
                    n0, n1 = (g % 2 * h.w // 2, (g % 2 + 1) * h.w // 2) if last else (0, h.w)
                    r = 124 if c < 2 else 123
                    mm = pe.matmul(psO[32 * g:32 * g + 32, n0:n1], vpad[j][0:r, c, :],
                                   probs[0:r, slot(j, c // 2), c % 2, n0:n1], start=(rnd == 0), stop=last,
                                   skip_group_check=True)
                mm.then_inc(pv_rounds, 1)

            def turn(h, j, u, c, t):
                r, m, first = (124 if u == 0 else 123), h.rows(t), 2 * u + c
                return pe.transpose(psS[0:r, pair(j, u) + c, t * P:t * P + m],
                                    big[0:m, j, t, first:first + T * (r - 1) + 1:T], ident[0:m, 0:m])

            def step(h, k, j, before, after):
                i, jn = 2 * k + j, 1 - j
                q = 0
                if after:
                    nh, ni = after
                    pe.wait_ge(kq_in[jn], 96 * h.turn(k + j) + 96)
                    while q < nh.early:
                        score(nh, ni, jn, q)
                        q += 1
                for u in range(UNITS):
                    pe.wait_ge(exp_done, h.exps(i) + u - 1)
                    if u == 0:
                        pe.wait_ge(sub_pool, h.subs("pool", i + 1))
                        pe.wait_ge(sub_act, h.subs("act", i + 1) - 1)
                        if not h.last:
                            pe.wait_ge(sub_dve, h.subs("dve", i + 1) - 1)
                        for c in range(2):
                            for t in range(h.nt - 1):
                                turn(h, j, u, c, t)
                        pe.wait_ge(sub_act, h.subs("act", i + 1))
                        pe.wait_ge(sub_dve, h.subs("dve", i + 1))
                        if h.last:
                            settle(pe)
                    for c in range(2):
                        for t in range(h.nt - 1 if u == 0 else 0, h.nt):
                            mm = turn(h, j, u, c, t)
                        if c == 1:
                            mm.then_inc(turned, 1)
                        while after and q < min(nh.units, -(-(2 * u + c + 1) * nh.units // nh.spread)):
                            score(nh, ni, jn, q)
                            q += 1
                    if u < 2 and before:
                        values(*before, jn, ROUNDS - 2 + u)
                    if u >= 3 and u % 2:
                        values(h, i, j, (u - 3) // 2)

            def last_values(h):
                values(h, HEADS - 1, 1, ROUNDS - 2)
                values(h, HEADS - 1, 1, ROUNDS - 1)

            pipeline(pe, first_scores, step, last_values)

            pe.wait_ge(o_kept, NB * HEADS + 1)
            for t in range(T):
                if t >= 2:
                    pe.wait_ge(f_kept, 2 * (t - 1))
                pe.wait_ge(f_mixed, t + 1)
                for hh in range(HD):
                    mm = pe.transpose(psS[:, 2 * (t % 2) + hh // 4, hh % 4 * P:hh % 4 * P + P], mix[t % 2][:, hh, :],
                                      ident[:, :])
                mm.then_inc(f_turned, 1)
                pe.wait_ge(f_kept, 2 * t + 2)
                if t >= 3:
                    pe.wait_ge(f_added, t - 2)
                for hh in range(HD):
                    mm = pe.matmul(psP[:, t % 3, 0:P], mixT[t % 2][:, hh, :], woR[:, hh, :], start=(hh == 0),
                                   stop=(hh == HD - 1))
                mm.then_inc(f_made, 1)

            turn_features(2)
            pe.wait_ge(xt_kept, 3 * NB)
            pe.wait_ge(f_added, T)
            for t in range(T):
                if t >= 3:
                    pe.wait_ge(y3_biased, t - 2)
                pe.matmul(psP[:, t % 3, 0:P], xT[:, t * P:(t + 1) * P], w3T[:, :], start=True, stop=True)\
                    .then_inc(y3_made, 1)
            product(3, [])

        @block.scalar
        def _(act):
            for n, (_, dst) in enumerate(w_jobs()):
                act.wait_ge(w_turned, n + 1)
                act.activation(dst, psS[:, n % 4, 0:P], ACT.Copy).then_inc(w_kept, 1)
            act.wait_ge(deg, 1)
            act.activation(stat[:, 1, :], stat[:, 0, :], ACT.Sqrt).then_inc(deg, 1)

            def product(L):
                g = gp[L]
                for b in range(NB):
                    w = tiles_of(b) * P
                    for c in range(0, T, 2):
                        gc = b * T + c
                        act.wait_ge(g["tr"], gc + 1)
                        if gc >= 4:
                            act.wait_ge(g["mm"], gc - 3)
                        act.activation(aT[:, gc % 4, 0:w], psS[:, gc % 4, 0:w], ACT.Copy).then_inc(g["act"], 1)
                    act.wait_ge(g["g"], b + 1)
                    if b >= 2:
                        act.wait_ge(g["out"], BT * (b - 1))
                    act.activation(gs[:, b % 2, 0:w], psO[:, 0:w], ACT.Copy).then_inc(g["gs"], 1)

            def norm(n):
                act.wait_ge(ln_var, n + 1)
                act.activation(stat[:, 3, :], stat[:, 2, :], ACT.Sqrt).then_inc(ln_std, 1)

            def keep_features(n):
                for q in range(NB):
                    w = tiles_of(q) * P
                    act.wait_ge(xt_turned, n * NB + q + 1)
                    act.activation(xT[:, q * BW:q * BW + w], psS[:, q % 4, 0:w], ACT.Copy).then_inc(xt_kept, 1)

            product(0)
            norm(0)
            keep_features(0)
            for made, kept, dst in ((h_made, h_kept, hT), (ad_made, ad_kept, adst_rows)):
                for q in range(NB):
                    w = tiles_of(q) * P
                    act.wait_ge(made, q + 1)
                    act.activation(dst[:, q * BW:q * BW + w], psP[:, q % 3, 0:w], ACT.Copy).then_inc(kept, 1)
            act.wait_ge(as_made, 1)
            act.activation(as_col[:, 0, :], psO[:, 0:T], ACT.Copy).then_inc(as_kept, 1)
            act.activation(as_col[:, 1, :], psO[:, 0:T], ACT.Copy, scale=0.2).then_inc(as_kept, 1)
            act.wait_ge(as_kept, 2)
            act.wait_ge(ad_kept, NB)
            for s in range(2 * T):
                half, t = divmod(s, T)
                if s >= 2:
                    act.wait_ge(gat_mm, s - 1)
                cols = adst_rows[:, half * HALF:(half + 1) * HALF]
                act.activation(gat_e[:, 2 * (s % 2), 0:HALF], cols, ACT.Exp, bias=as_col[:, 0, t:t + 1])\
                    .then_inc(e_ready, 1)
                act.activation(gat_e[:, 2 * (s % 2) + 1, 0:HALF], cols, ACT.Exp, bias=as_col[:, 1, t:t + 1],
                               scale=0.2).then_inc(e_ready, 1)
            norm(1)
            keep_features(1)
            for t in range(T):
                j = t % 2
                for which in range(2):
                    act.wait_ge(pj_made, 3 * t + which + 1)
                    src = psS[:, 2 * which:2 * which + 2, :].rearrange("p a (c h) -> p h a c", h=HD)
                    scale = 0.5 * float(P) ** -0.5 if which == 0 else 1.0
                    if t:
                        act.wait_ge(pj_dve, 4 * (t - 1) + 2 * which + 2)
                    if t >= 2:
                        act.wait_ge(pj_out[j], 7 * 16 * (t // 2))
                    act.activation(scaled[which].rearrange("p (h a c) -> p h a c", h=HD, a=2), src, ACT.Copy,
                                   scale=scale).then_inc(pj_act, 1)
                    act.activation(parts[2 * j + which][:, 0, :].rearrange("p (h a c) -> p h a c", h=HD, a=2), src,
                                   ACT.Copy, scale=scale).then_inc(pj_act, 1)
                    act.wait_ge(pj_dve, 4 * t + 2 * which + 1)
                    act.activation(parts[2 * j + which][:, 1, :], rest[which], ACT.Copy).then_inc(pj_act, 1)

            def subtract(h, i, j, piece):
                t, half = h.pieces("act")[piece]
                act.wait_ge(max_ready, h.maxes(i) + t + 1)
                r = h.rows(t)
                part = big[0:r, j, t, half * HALF:(half + 1) * HALF]
                act.activation(part, part, ACT.Identity, bias=neg_max[0:r, j, t:t + 1]).then_inc(sub_act, 1)

            def first_subtract(h):
                for piece in range(len(h.pieces("act"))):
                    subtract(h, 0, 0, piece)

            def keep_sums(h, i, j, turns):
                act.wait_ge(pv_rounds, ROUNDS * h.it(i) + 2 * ROUNDS)
                act.wait_ge(o_out[j], 64 * turns + 1)
                act.activation(obuf[j][:, 0:h.w], psO[:, 0:h.w], ACT.Copy).then_inc(o_kept, 1)

            def step(h, k, j, before, after):
                i = 2 * k + j
                at = {5: 0, 9: 1}
                for u in range(UNITS):
                    r = 124 if u == 0 else 123
                    act.wait_ge(turned, h.turns(i) + u + 1)
                    act.wait_ge(pv_rounds, ROUNDS * h.it(i) + slot_free(j, u))
                    act.activation(probs[0:r, slot(j, u), :, 0:h.w], psS[0:r, pair(j, u):pair(j, u) + 2, 0:h.w],
                                   ACT.Exp, scale=2.0).then_inc(exp_done, 1)
                    if u == 1 and before:
                        keep_sums(*before, 1 - j, h.turn(k + j - 1))
                    if after and u in at:
                        subtract(*after, 1 - j, at[u])

            def last_sums(h):
                keep_sums(h, HEADS - 1, 1, h.turn(HEADS // 2 - 1))

            pipeline(act, first_subtract, step, last_sums)

            for t in range(T):
                act.wait_ge(f_turned, t + 1)
                if t >= 2:
                    act.wait_ge(f_made, t - 1)
                for a in range(2):
                    act.activation(mixT[t % 2][:, 4 * a:4 * a + 4, :].rearrange("p h c -> p (h c)"),
                                   psS[:, 2 * (t % 2) + a, :], ACT.Copy).then_inc(f_kept, 1)
            norm(2)
            keep_features(2)
            product(3)
            norm(3)

        @block.gpsimd
        def _(pool):
            pool.memset(ones[:, :], 1.0).then_inc(cleared, 1)
            pool.memset(xn[:, T - 1, :], 0.0).then_inc(cleared, 1)
            pool.wait_ge(gat_div, 2 * HC)
            pool.memset(mem[64:96, K_AT:VR_AT], 0.0).then_inc(at_clear, 1)
            pool.wait_ge(at_clear, 1)
            pool.memset(vpad_all, 0.0).then_inc(at_clear, 1)
            pool.wait_ge(at_clear, 2)
            pool.memset(vpad_all.rearrange("p (t c) -> p t c", c=32)[:, :, HD:HD + 1], 1.0).then_inc(at_clear, 1)
            pool.wait_ge(at_clear, 3)

            def pad_values(h, i, k, j):
                pool.wait_ge(v_in[j], 16 * h.turn(k) + 16)
                settle(pool)
                pool.tensor_copy(vpad[j][0:124, :, 0:HD], vraw[j][0:124, :, :]).then_inc(v_padded, 1)

            def subtract(h, i, j):
                for t, half in h.pieces("pool"):
                    pool.wait_ge(max_ready, h.maxes(i) + t + 1)
                    part = big[:, j, t, half * HALF:(half + 1) * HALF]
                    pool.tensor_tensor(part, part, neg_max[:, j, t:t + 1].broadcast_to([P, HALF]), ALU.add)\
                        .then_inc(sub_pool, 1)

            def first(h):
                pool.wait_ge(pv_rounds, ROUNDS * h.it(0) + ROUNDS)
                pad_values(h, 0, 0, 0)
                subtract(h, 0, 0)

            def step(h, k, j, before, after):
                i, jn = 2 * k + j, 1 - j
                if after:
                    pool.wait_ge(pv_rounds, ROUNDS * h.it(i) + ROUNDS)
                    pad_values(h, i + 1, k + j, jn)
                    subtract(*after, jn)

            pipeline(pool, first, step)

        @block.vector
        def _(dve):
            for b in range(NB):
                dve.wait_ge(rs_in[b % 2], 32 * (b // 2 + 1))
                for t in range(tiles_of(b)):
                    dve.tensor_reduce(rowsum[:, BT * b + t:BT * b + t + 1], big[:, b % 2, t, 0:N], AX.X, ALU.add)\
                        .then_inc(rs_done, 1)
            dve.wait_ge(rs_done, T)
            steps = [0]

            def chained(ins):
                steps[0] += 1
                ins.then_inc(ln_step, 1)
                dve.wait_ge(ln_step, steps[0])

            chained(dve.tensor_scalar(rowsum[:, :], rowsum[:, :], 1.0, None, ALU.add))
            dve.tensor_scalar(stat[:, 0, :], rowsum[:, :], 1e-30, None, ALU.max).then_inc(deg, 1)
            dve.wait_ge(deg, 2)
            chained(dve.reciprocal(dinv[:, :], stat[:, 1, :]))
            chained(dve.tensor_scalar(stat[:, 4, :], rowsum[:, :], 0.0, None, ALU.is_gt))
            chained(dve.tensor_tensor(dinv3[:, :], dinv[:, :], stat[:, 4, :], ALU.mult))

            def by_node(ap):
                return ap.unsqueeze(2).broadcast_to([P, T, P])

            def product(L):
                g = gp[L]
                for b in range(NB):
                    w = tiles_of(b) * P
                    for c in range(1, T, 2):
                        gc = b * T + c
                        dve.wait_ge(g["tr"], gc + 1)
                        if gc >= 4:
                            dve.wait_ge(g["mm"], gc - 3)
                        dve.tensor_copy(aT[:, gc % 4, 0:w], psS[:, gc % 4, 0:w]).then_inc(g["dve"], 1)
                    for t in range(tiles_of(b)):
                        n = BT * b + t
                        dve.wait_ge(g["out"], n + 1)
                        if L == 0:
                            ins = dve.scalar_tensor_tensor(out=z[:, n, :], in0=psP[:, n % 3, 0:P],
                                                           scalar=dinv[:, n:n + 1], in1=b0r[:, :],
                                                           op0=ALU.mult, op1=ALU.add)
                        else:
                            ins = dve.tensor_scalar(z[:, n, :], psP[:, n % 3, 0:P], dinv3[:, n:n + 1], None, ALU.mult)
                        ins.then_inc(g["z"], 1)
                dve.wait_ge(g["z"], T)
                chained(dve.scalar_tensor_tensor(out=z[:, :, :], in0=z[:, :, :], scalar=0.0, in1=xn[:, :, :],
                                                 op0=ALU.max, op1=ALU.add))

            def norm(n):
                chained(dve.tensor_reduce(stat[:, 0, :], z[:, :, :], AX.X, ALU.add))
                chained(dve.tensor_scalar(stat[:, 1, :], stat[:, 0, :], 1.0 / P, None, ALU.mult))
                chained(dve.tensor_tensor(z[:, :, :], z[:, :, :], by_node(stat[:, 1, :]), ALU.subtract))
                chained(dve.tensor_tensor(xn[:, :, :], z[:, :, :], z[:, :, :], ALU.mult))
                chained(dve.tensor_reduce(stat[:, 0, :], xn[:, :, :], AX.X, ALU.add))
                dve.tensor_scalar(stat[:, 2, :], stat[:, 0, :], 1.0 / P, EPS, ALU.mult, ALU.add).then_inc(ln_var, 1)
                dve.wait_ge(ln_std, n + 1)
                chained(dve.reciprocal(stat[:, 5, :], stat[:, 3, :]))
                dve.tensor_tensor(xn[:, :, :], z[:, :, :], by_node(stat[:, 5, :]), ALU.mult).then_inc(ln_x, 1)

            dve.wait_ge(in_x, 32)
            dve.wait_ge(in_small, 96)
            dve.wait_ge(cleared, 2)
            dve.tensor_tensor(z_or_y(0), xn[:, :, :], by_node(dinv[:, :]), ALU.mult).then_inc(gp[0]["y"], 1)
            product(0)
            norm(0)

            dve.tensor_scalar(dst_rep[:, :], ones[:, :], adst[:, 0:1], None, ALU.mult).then_inc(dst_ready, 1)
            for q in range(NB):
                w = tiles_of(q)
                dve.wait_ge(hn_made, q + 1)
                dve.tensor_copy(hn[:, BT * q:BT * q + w, :].rearrange("p t f -> p (t f)"), psS[:, q % 4, 0:w * P])\
                    .then_inc(hn_kept, 1)
            made = 0
            loads = 0
            for s in range(2 * T):
                half, t = divmod(s, T)
                b, tb = divmod(t, BT)
                slot = b % 2
                if tb == 0:
                    dve.wait_ge(gat_in[slot], 32 * (half * (NB // 2) + b // 2 + 1))
                e1, e2 = gat_e[:, 2 * (s % 2), 0:HALF], gat_e[:, 2 * (s % 2) + 1, 0:HALF]
                rows = big[:, slot, tb, 0:HALF]
                dve.wait_ge(e_ready, 2 * s + 2)
                dve.tensor_tensor(e1, e1, e2, ALU.max).then_inc(gat_w, 1)
                dve.wait_ge(gat_w, 3 * s + 1)
                dve.tensor_tensor(e1, e1, rows, ALU.mult).then_inc(gat_w, 1)
                dve.wait_ge(gat_w, 3 * s + 2)
                dve.tensor_tensor(e2, e1, rows, ALU.mult).then_inc(gat_w, 1)
                if t == T - 1:
                    dve.wait_ge(gat_mm, s + 1)
                    rec = z[:, :, :].rearrange("p t f -> p (t f)")
                    for c in range(HC):
                        w = min(CW, HALF - c * CW)
                        dve.reciprocal(rec[:, c * CW:c * CW + w], psS[:, c, 0:w]).then_inc(gat_rcp, 1)
                    for c in range(HC):
                        w = min(CW, HALF - c * CW)
                        dve.wait_ge(gat_rcp, HC * half + c + 1)
                        dve.tensor_tensor(xT[:, half * HALF + c * CW:half * HALF + c * CW + w], psP[:, c, 0:w],
                                          rec[:, c * CW:c * CW + w], ALU.mult).then_inc(gat_div, 1)
            for q in range(NB):
                w = tiles_of(q)
                dve.wait_ge(gz_turned, q + 1)
                dve.tensor_tensor(z[:, BT * q:BT * q + w, :], psS[:, q % 4, 0:w * P].rearrange("p (t f) -> p t f", f=P),
                                  xn[:, BT * q:BT * q + w, :], ALU.add).then_inc(gz_added, 1)
            dve.wait_ge(gz_added, NB)
            norm(1)

            dve.memset(zero_row, 0.0).then_inc(pj_zero, 1)
            for t in range(T):
                j = t % 2
                for which in range(2):
                    part = parts[2 * j + which]
                    dve.wait_ge(pj_act, 6 * t + 3 * which + 2)
                    dve.tensor_tensor(rest[which], scaled[which], part[:, 0, :], ALU.subtract).then_inc(pj_dve, 1)
                    dve.wait_ge(pj_act, 6 * t + 3 * which + 3)
                    dve.wait_ge(pj_dve, 4 * t + 2 * which + 1)
                    dve.tensor_tensor(part[:, 2, :], rest[which], part[:, 1, :], ALU.subtract).then_inc(pj_dve, 1)
                dve.wait_ge(pj_made, 3 * t + 3)
                if t >= 2:
                    dve.wait_ge(pj_out[j], 7 * 16 * (t // 2))
                ins = dve.tensor_copy(v_out[j].rearrange("p (a n) -> p a n", a=2), psP[:, 0:2, :])
                ins.then_inc(pj_taken, 1)
            for j in range(2):
                dve.wait_ge(pj_out[j], 7 * 16 * (T // 2))
            dve.wait_ge(pj_tail, 16)
            dve.sem_inc(taken, 4)
            for s in (scored, exp_done, o_kept, turned, v_padded, *o_out):
                dve.sem_inc(s, 1)
            dve.sem_inc(exp_done, 1)
            dve.sem_inc(pv_rounds, ROUNDS)
            dve.sem_inc(turned, UNITS)

            def score_max(h, i, j, new_rows=False):
                units = h.units
                for q in range(units + 1):
                    if q < units:
                        t, c = divmod(q, NC)
                        r, w = h.rows(t), chunk(c)
                        if new_rows and c == 0:
                            dve.wait_ge(adj_in[t], 16 * (h.b + 1))
                        dve.wait_ge(scored, h.scored(i) + q + 1)
                        settle(dve)
                        dve.tensor_tensor_reduce(big[0:r, j, t, c * CW:c * CW + w], psP[0:r, q % 3, 0:w],
                                                 adj_rows[0:r, t, c * CW:c * CW + w], 1.0, LOWEST, ALU.add, ALU.max,
                                                 part_max[0:r, j, t, c:c + 1]).then_inc(taken, 1)
                    if q and q % NC == 0:
                        t = q // NC - 1
                        r = h.rows(t)
                        dve.wait_ge(taken, h.scored(i) + q + 3)
                        dve.tensor_reduce(neg_max[0:r, j, t:t + 1], part_max[0:r, j, t, :], AX.X, ALU.max,
                                          negate=True).then_inc(max_ready, 1)
                    for t, half in h.pieces("dve"):
                        if q == min(NC * (t + 1) + 1, units):
                            r = h.rows(t)
                            dve.wait_ge(max_ready, h.maxes(i) + t + 1)
                            part = big[0:r, j, t, half * HALF:(half + 1) * HALF]
                            dve.tensor_scalar(part, part, neg_max[0:r, j, t:t + 1], None, ALU.add)\
                                .then_inc(sub_dve, 1)

            def first_scores(h):
                dve.wait_ge(turned, h.turns(-1))
                score_max(h, 0, 0, new_rows=True)

            def step(h, k, j, first, has_next):
                i = 2 * k + j
                if has_next:
                    dve.wait_ge(turned, h.turns(i))
                    score_max(h, i + 1, 1 - j)

            with dve.Fori(0, FULL) as b:
                blocks_of_heads(dve, Head(b, False), first_scores, step)
            blocks_of_heads(dve, Head(FULL, True), first_scores, step)

            for t in range(T):
                j = t % 2
                if t < 2:
                    dve.wait_ge(turned, UNITS * (NB * HEADS + 1) + 1)
                dve.wait_ge(f_in[j], 64 * (t // 2 + 1))
                f = [fin[j][:, g, :, :] for g in range(4)]
                chained(dve.tensor_tensor(f[0], f[0], f[1], ALU.add))
                chained(dve.tensor_tensor(f[2], f[2], f[3], ALU.add))
                chained(dve.tensor_tensor(f[0], f[0], f[2], ALU.add))
                chained(dve.reciprocal(rden[j], fin[j][:, 0, HD, :]))
                if t >= 2:
                    dve.wait_ge(f_turned, t - 1)
                dve.tensor_tensor(mix[j], fin[j][:, 0, 0:HD, :], rden[j].unsqueeze(1).broadcast_to([P, HD, P]),
                                  ALU.mult).then_inc(f_mixed, 1)
                if t:
                    dve.wait_ge(f_made, t)
                    dve.tensor_tensor(z[:, t - 1, :], psP[:, (t - 1) % 3, 0:P], xn[:, t - 1, :], ALU.add)\
                        .then_inc(f_added, 1)
            dve.wait_ge(f_made, T)
            dve.tensor_tensor(z[:, T - 1, :], psP[:, (T - 1) % 3, 0:P], xn[:, T - 1, :], ALU.add).then_inc(f_added, 1)
            dve.wait_ge(f_added, T)
            norm(2)

            y3 = z_or_y(3)
            for t in range(T):
                dve.wait_ge(y3_made, t + 1)
                dve.tensor_tensor(z[:, t, :], psP[:, t % 3, 0:P], b3r[:, :], ALU.add).then_inc(y3_biased, 1)
            dve.wait_ge(y3_biased, T)
            dve.tensor_tensor(y3, z[:, :, :], by_node(dinv3[:, :]), ALU.mult).then_inc(gp[3]["y"], 1)
            product(3)
            norm(3)


_INS = ["x", "adj", "L0_gnn_W", "L0_gnn_b", "L1_gnn_weight", "L1_gnn_att_src", "L1_gnn_att_dst", "L2_gnn_Wq",
        "L2_gnn_Wk", "L2_gnn_Wv", "L2_gnn_Wo", "L3_gnn_W", "L3_gnn_b"]


def kernel(**inputs):
    import numpy as _np
    import concourse.bacc as _bacc
    from concourse import mybir as _mybir
    from concourse.bass_utils import run_bass_kernel_spmd as _run

    nc = _bacc.Bacc("TRN2", target_bir_lowering=False, num_devices=1)
    arrays, args = {}, []
    for name in _INS:
        a = _np.ascontiguousarray(inputs[name])
        arrays[f"in_{name}"] = a
        args.append(nc.dram_tensor(f"in_{name}", a.shape, _mybir.dt.from_np(a.dtype), kind="ExternalInput").ap())
    arrays["identity"] = _np.eye(P, dtype=_np.float32)
    args.append(nc.dram_tensor("identity", (P, P), F32, kind="ExternalInput").ap())
    out = nc.dram_tensor("out_0", (N, P), F32, kind="ExternalOutput").ap()
    program(nc, *args, out)
    r = _run(nc, [arrays], core_ids=[0])
    return r.results[0]["out_0"]
```
